# Optimizing a Trainium2 kernel written in Bass

```python
import numpy as np
import jax
import jax.numpy as jnp

def _softmax(x, axis=-1):
    return jax.nn.softmax(x, axis=axis)

def _gelu(x):
    return jax.nn.gelu(x, approximate=True)

def _silu(x):
    return jax.nn.silu(x)

def _sigmoid(x):
    return jax.nn.sigmoid(x)

def _layernorm(x, axis=-1, eps=1e-05):
    m = jnp.mean(x, axis=axis, keepdims=True)
    v = jnp.var(x, axis=axis, keepdims=True)
    return (x - m) / jnp.sqrt(v + eps)

def _scatter_add(tgt, idx, src, axis=0):
    return tgt.at[idx].add(src)

def _segment_sum(src, seg, n):
    return jax.ops.segment_sum(src, seg, n)
kernel_name = 'mk_adj_ffn_d1_adj_r2_e88384'

def setup_inputs(seed: int=0):
    np.random.seed(seed)
    _w = jnp.asarray

    def _rec_inputs():
        import jax
        import jax.numpy as jnp
        _gk = jax.random.key(seed)
        x = -0.0005146 + 1 * jax.random.normal(jax.random.fold_in(_gk, 1), (8, 1024, 128), jnp.float32)
        _a = jax.random.bernoulli(jax.random.fold_in(_gk, 2), 0.015625, (8, 1024, 1024))
        adj = _a.astype(jnp.int32)
        return (x, adj)
    x, adj = _rec_inputs()

    def _L0_gnn_setup():
        import jax, jax.numpy as jnp
        import numpy as np
        B, N, C, OUT, S = (4, 1024, 128, 128, 25)
        DENSITY = 0.008
        key = jax.random.key(seed)
        kA, kX, kW = jax.random.split(key, 3)
        A = jax.random.bernoulli(kA, DENSITY, (B, N, N)).astype(jnp.int32)
        X = jax.random.normal(kX, (B, N, C), dtype=jnp.float32)
        W = jax.random.normal(kW, (2 * C, OUT), dtype=jnp.float32) * np.float32(1.0 / np.sqrt(2 * C))
        b = jnp.zeros((OUT,), dtype=jnp.float32)
        return {'A': A, 'X': X, 'W': W, 'b': b}
    _L0_gnn_all = _L0_gnn_setup()
    _L0_gnn_in = {k: v for k, v in _L0_gnn_all.items() if k in ('W', 'b')}
    del _L0_gnn_all

    def _L0_ffn_setup():
        import jax, jax.numpy as jnp
        import numpy as np
        B, S, H, F, E, K = (8, 2048, 128, 256, 16, 2)
        EPS = 1e-05
        key = jax.random.key(seed)
        ks = jax.random.split(key, 9)
        sc = 0.02
        return {'x': jax.random.normal(ks[0], (B, S, H), dtype=jnp.float32), 'gate_w': jax.random.normal(ks[1], (H, E), dtype=jnp.float32) * sc, 'gate_b': jnp.zeros((E,), dtype=jnp.float32), 'w1': jax.random.normal(ks[2], (E, H, F), dtype=jnp.float32) * sc, 'b1': jnp.zeros((E, F), dtype=jnp.float32), 'w2': jax.random.normal(ks[3], (E, F, H), dtype=jnp.float32) * sc, 'b2': jnp.zeros((E, H), dtype=jnp.float32), 'gamma': jnp.ones((H,), dtype=jnp.float32), 'beta': jnp.zeros((H,), dtype=jnp.float32)}
    _L0_ffn_all = _L0_ffn_setup()
    _L0_ffn_in = {k: v for k, v in _L0_ffn_all.items() if k in ('gate_w', 'gate_b', 'w1', 'b1', 'w2', 'b2', 'gamma', 'beta')}
    del _L0_ffn_all
    return {'x': x, 'adj': adj, 'L0_gnn_W': _L0_gnn_in['W'], 'L0_gnn_b': _L0_gnn_in['b'], 'L0_ffn_gate_w': _L0_ffn_in['gate_w'], 'L0_ffn_gate_b': _L0_ffn_in['gate_b'], 'L0_ffn_w1': _L0_ffn_in['w1'], 'L0_ffn_b1': _L0_ffn_in['b1'], 'L0_ffn_w2': _L0_ffn_in['w2'], 'L0_ffn_b2': _L0_ffn_in['b2'], 'L0_ffn_gamma': _L0_ffn_in['gamma'], 'L0_ffn_beta': _L0_ffn_in['beta']}

def reference(x, adj, L0_gnn_W, L0_gnn_b, L0_ffn_gate_w, L0_ffn_gate_b, L0_ffn_w1, L0_ffn_b1, L0_ffn_w2, L0_ffn_b2, L0_ffn_gamma, L0_ffn_beta):
    import jax
    import jax.numpy as jnp

    def _L0_gnn_ref(A, X, W, b):
        import jax, jax.numpy as jnp
        import numpy as np
        B, N, C, OUT, S = (4, 1024, 128, 128, 25)
        DENSITY = 0.008
        mask = A != 0
        neg_inf = jnp.float32(-jnp.inf)
        pri = -jnp.arange(N, dtype=jnp.float32)
        scores = jnp.where(mask, pri, neg_inf)
        vals, idx = jax.lax.top_k(scores, S)
        valid = vals > neg_inf
        feats = jax.vmap(lambda x, i: x[i])(X, idx)
        feats = jnp.where(valid[..., None], feats, neg_inf)
        agg = feats.max(axis=2)
        degree = mask.sum(axis=-1)
        agg = jnp.where((degree <= S)[..., None], jnp.maximum(agg, 0.0), agg)
        h = jnp.concatenate([X, agg], axis=-1)
        out = jax.nn.relu(jnp.einsum('bnf,fo->bno', h, W) + b)
        return out

    def _L0_ffn_ref(x, gate_w, gate_b, w1, b1, w2, b2, gamma, beta):
        import jax, jax.numpy as jnp
        import numpy as np
        B, S, H, F, E, K = (8, 2048, 128, 256, 16, 2)
        EPS = 1e-05
        gate_logits = x @ gate_w + gate_b
        topk_vals, topk_idx = jax.lax.top_k(gate_logits, K)
        topk_w = jax.nn.softmax(topk_vals, axis=-1)
        h = jax.nn.relu(jnp.einsum('bsh,ehf->bsef', x, w1) + b1)
        expert_out = jnp.einsum('bsef,efh->bseh', h, w2) + b2
        sel = jnp.take_along_axis(expert_out, topk_idx[:, :, :, None], axis=2)
        moe = jnp.sum(topk_w[..., None] * sel, axis=2)
        y = x + moe
        mu = jnp.mean(y, axis=-1, keepdims=True)
        var = jnp.var(y, axis=-1, keepdims=True)
        return (y - mu) / jnp.sqrt(var + EPS) * gamma + beta
    x = x + _L0_gnn_ref(adj, _layernorm(x, axis=-1), L0_gnn_W, L0_gnn_b)
    x = x + _L0_ffn_ref(_layernorm(x, axis=-1), L0_ffn_gate_w, L0_ffn_gate_b, L0_ffn_w1, L0_ffn_b1, L0_ffn_w2, L0_ffn_b2, L0_ffn_gamma, L0_ffn_beta)
    return x

_drawn_inputs = setup_inputs


def setup_inputs(seed=0):
    import zlib

    import numpy as np

    out = dict(_drawn_inputs(seed))
    spreads = {'L0_gnn_b': (0.0, 0.1),
     'L0_ffn_gate_b': (0.0, 0.27),
     'L0_ffn_b1': (0.0, 0.8),
     'L0_ffn_b2': (0.0, 0.286),
     'L0_ffn_gamma': (1.0, 0.2),
     'L0_ffn_beta': (0.0, 0.1)}
    factors = {'L0_ffn_w1': 3.987, 'L0_ffn_w2': 3.149}
    for name, (base, spread) in spreads.items():
        noise = np.random.default_rng([zlib.crc32(name.encode()), seed]).standard_normal(out[name].shape)
        drawn = base * np.exp(spread * noise) if base else spread * noise
        out[name] = jnp.asarray(drawn.astype(out[name].dtype))
    for name, factor in factors.items():
        out[name] = (out[name] * factor).astype(out[name].dtype)
    return out
```

```python
from contextlib import ExitStack

import numpy as np

import concourse.bass as bass
from concourse import mybir

F32 = mybir.dt.float32
F16 = mybir.dt.float16
I32 = mybir.dt.int32
U32 = mybir.dt.uint32
ALU = mybir.AluOpType
ACT = mybir.ActivationFunctionType
AX = mybir.AxisListType

P = 128
B, N, C = 8, 1024, 128
S = 25
E, F = 16, 256
FC = F // P
TILES = B * N // P
GT = 4
GROUPS = TILES // GT
BT = N // P
GB = BT // GT
ROWS = N + 1
EPS = 1e-5
LOWEST = -3.0e38
TOP = 8
ROUNDS = -(-(S + 1) // TOP)


def shape_constants():
    first = np.zeros((P, 2 * P), np.float32)
    first[:, :P] = np.eye(P)
    first[:, P:P + E] = np.arange(E)
    first[:, P + E:P + E + GROUPS] = (np.arange(GROUPS) // GB) * ROWS + N
    priority = np.broadcast_to((N - np.arange(N)).astype(np.float16), (P, N))
    return {"small": first, "priority": np.ascontiguousarray(priority)}


def build(nc, x, adj, W, b, gate_w, gate_b, w1, b1, w2, b2, gamma, beta, small, priority, out):
    with ExitStack() as ctx:
        def sb(name, shape, dt=F32):
            return ctx.enter_context(nc.sbuf_tensor(name, shape, dt))

        def ps(name, shape, dt=F32):
            return ctx.enter_context(nc.psum_tensor(name, shape, dt))

        def sem(name):
            return ctx.enter_context(nc.semaphore(name))

        table = nc.dram_tensor("gather_table", (B, ROWS, C), F32).ap()

        const = sb("const", [P, 2 * P])
        ident = const[:, 0:P]
        expert_ids = const[:, P:P + E]
        none_row = const[:, P + E:P + E + GROUPS]
        pri = sb("pri", [P, N], F16)
        W_sb = sb("W_sb", [P, 2, C])
        rows = sb("rows", [1, C + E])
        ones = sb("ones", [1, P])
        gw_sb = sb("gw_sb", [P, E])
        w1_sb = sb("w1_sb", [P, E, F])
        w2_sb = sb("w2_sb", [P, E, FC, C])
        b1_sb = sb("b1_sb", [P, E, FC])
        b2_sb = sb("b2_sb", [E, C])
        gamma_sb = sb("gamma_sb", [P, C])
        beta_sb = sb("beta_sb", [P, C])
        eps = sb("eps", [P, 1])
        zrow = sb("zrow", [B, C])

        x_sb = sb("x_sb", [P, TILES, C])
        n_sb = sb("n_sb", [P, TILES, C])

        nst = sb("nst", [P, BT, 6])
        nmv = sb("nmv", [P, BT, 2])
        nsd = sb("nsd", [P, BT])
        nrs = sb("nrs", [P, BT])

        adj_sb = sb("adj_sb", [P, GT, N], I32)
        score = sb("score", [P, N], F16)
        top = sb("top", [P, GT, ROUNDS * TOP])
        nbr = sb("nbr", [P, GT, S], I32)
        floor = sb("floor", [P, GT, 1])
        got = sb("got", [P, GT, S, C])
        n_grp = sb("n_grp", [P, GT, C])
        agg = sb("agg", [P, GT, C])
        nT = sb("nT", [P, GT, P])
        aggT = sb("aggT", [P, GT, P])
        x1 = sb("x1", [P, GT, C])
        m = sb("m", [P, GT, C])
        mT = sb("mT", [P, GT, P])
        st = sb("st", [P, GT, 6])
        mv = sb("mv", [P, GT, 2])
        sd = sb("sd", [P, GT])
        rs = sb("rs", [P, GT])
        logit = sb("logit", [P, GT, E])
        top2 = sb("top2", [P, GT, TOP])
        pick = sb("pick", [P, GT, TOP], U32)
        pickf = sb("pickf", [P, GT, 2])
        gap = sb("gap", [P, GT])
        eg = sb("eg", [P, GT])
        den = sb("den", [P, GT])
        wa = sb("wa", [P, GT])
        wb = sb("wb", [P, GT])
        ga = sb("ga", [P, GT, E])
        gb2 = sb("gb2", [P, GT, E])
        gate = sb("gate", [P, GT, E])
        gateT = sb("gateT", [E, GT, P])
        h_sb = sb("h_sb", [P, 2, FC, GT * P])
        y = sb("y", [P, GT, C])
        st2 = sb("st2", [P, GT, 6])
        mv2 = sb("mv2", [P, GT, 2])
        sd2 = sb("sd2", [P, GT])
        rs2 = sb("rs2", [P, GT])
        z = sb("z", [P, GT, C])
        xb = sb("xb", [P, GT, C])
        res = sb("res", [P, GT, C])

        turned = ps("turned", [P, GT, P])
        turned_agg = ps("turned_agg", [P, GT, P])
        lin = ps("lin", [P, GT, C])
        gates_ps = ps("gates_ps", [P, GT * P])
        h_ps = [ps(f"h_ps{f}", [P, GT * P]) for f in range(FC)]
        o_ps = [ps(f"o_ps{k}", [P, GT, C]) for k in range(2)]

        consts_in = sem("consts_in")
        x_in = sem("x_in")
        pool_ready = sem("pool_ready")
        adj_in = [sem(f"adj_in{a}") for a in range(GT)]
        gathered = [sem(f"gathered{a}") for a in range(GT)]
        table_zero = sem("table_zero")
        table_out = sem("table_out")
        out_stored = sem("out_stored")
        gathers_begun = sem("gathers_begun")
        norm_steps = sem("norm_steps")
        nstats_ready = sem("nstats_ready")
        norm_std = sem("norm_std")
        n_ready = sem("n_ready")
        adj_read = sem("adj_read")
        rank_steps = sem("rank_steps")
        nbr_ready = sem("nbr_ready")
        reduced = sem("reduced")
        agg_ready = sem("agg_ready")
        n_taken = sem("n_taken")
        nT_turned = sem("nT_turned")
        nT_ready = sem("nT_ready")
        aggT_turned = sem("aggT_turned")
        aggT_ready = sem("aggT_ready")
        lin_ready = sem("lin_ready")
        ffn_steps = sem("ffn_steps")
        x1_stats = sem("x1_stats")
        x1_std = sem("x1_std")
        m_ready = sem("m_ready")
        m_turned = sem("m_turned")
        mT_ready = sem("mT_ready")
        logit_ready = sem("logit_ready")
        gap_ready = sem("gap_ready")
        exp_ready = sem("exp_ready")
        gate_ready = sem("gate_ready")
        gate_turned = sem("gate_turned")
        gateT_ready = sem("gateT_ready")
        bias_ready = sem("bias_ready")
        h_ready = sem("h_ready")
        relu_ready = sem("relu_ready")
        o_ready = sem("o_ready")
        o_used = sem("o_used")
        y_stats = sem("y_stats")
        y_std = sem("y_std")
        res_ready = sem("res_ready")

        x_t = x.rearrange("b (t p) c -> p (b t) c", p=P)
        out_g = out.rearrange("b (g a p) c -> (b g) p a c", p=P, a=GT)
        adj_g = adj.rearrange("b (g a p) j -> (b g) a p j", p=P, a=GT)
        table_b = table[:, 0:N, :].rearrange("b (t p) c -> b p t c", p=P)
        table_rows = table.rearrange("b r c -> (b r) c")

        block = ctx.enter_context(nc.Block())

        CONST_LOADS = 12

        @block.sync
        def _(sp):
            sp.dma_start(x_sb[:], x_t).then_inc(x_in, 16)
            for dst, src in ((const[:], small), (pri[:], priority)):
                sp.dma_start(dst, src).then_inc(consts_in, 16)
            for a in range(GT):
                sp.dma_start(adj_sb[:, a, :], adj_g[0, a]).then_inc(adj_in[a], 16)
            for dst, src in (
                (W_sb[:], W.rearrange("(k p) o -> p k o", p=P)),
                (rows[:, 0:C], b.rearrange("(a c) -> a c", a=1)),
                (rows[:, C:C + E], gate_b.rearrange("(a c) -> a c", a=1)),
                (gw_sb[:], gate_w),
                (w1_sb[:], w1.rearrange("e p f -> p e f")),
                (w2_sb[:], w2.rearrange("e (k p) c -> p e k c", p=P)),
                (b1_sb[:], b1),
                (b2_sb[:], b2),
                (gamma_sb[:], gamma.partition_broadcast(P)),
                (beta_sb[:], beta.partition_broadcast(P)),
            ):
                sp.dma_start(dst, src).then_inc(consts_in, 16)
            sp.sem_inc(out_stored, 16)
            sp.wait_ge(pool_ready, 1)
            sp.dma_start(table[:, N, :], zrow[:]).then_inc(table_zero, 16)
            for g in range(B):
                sp.wait_ge(n_ready, g + 1)
                sp.dma_start(table_b[g], n_sb[:, g * BT:(g + 1) * BT, :]).then_inc(table_out, 16)

            with sp.Fori(0, GROUPS - 1) as i:
                for a in range(GT):
                    sp.wait_ge(adj_read, i * GT + (a + 1))
                    sp.dma_start(adj_sb[:, a, :], adj_g[i + 1, a]).then_inc(adj_in[a], 16)
                sp.wait_ge(res_ready, i + 1)
                sp.dma_start(out_g[i], res[:]).then_inc(out_stored, 16)
            sp.wait_ge(res_ready, GROUPS)
            sp.dma_start(out_g[GROUPS - 1], res[:]).then_inc(out_stored, 16)
            sp.wait_ge(out_stored, 16 * (GROUPS + 1))
            sp.wait_ge(table_zero, 16)
            sp.wait_ge(table_out, 16 * B)

        @block.gpsimd
        def _(pool):
            pool.memset(zrow[:], 0.0).then_inc(pool_ready, 1)
            pool.memset(ones[:], 1.0).then_inc(pool_ready, 1)
            pool.memset(eps[:], EPS).then_inc(pool_ready, 1)
            pool.wait_ge(table_out, 16 * B)
            pool.wait_ge(table_zero, 16)
            with pool.Fori(0, GROUPS) as i:
                for a in range(GT):
                    pool.wait_ge(nbr_ready, i * GT + (a + 1))
                    pool.sem_inc(gathers_begun, 1)
                    for k in range(S):
                        pool.indirect_dma_start(
                            out=got[:, a, k, :], out_offset=None, in_=table_rows,
                            in_offset=bass.IndirectOffsetOnAxis(ap=nbr[:, a, k:k + 1], axis=0),
                        ).then_inc(gathered[a], 16)

        @block.vector
        def _(dve):
            v = nc.vector
            dve.wait_ge(consts_in, 16 * CONST_LOADS)

            dve.wait_ge(x_in, 16)
            with dve.Fori(0, B) as g:
                tiles = [bass.ds(g * BT + t, 1) for t in range(BT)]
                dve.sem_clear(norm_steps)
                for t in range(BT):
                    last = v.bn_stats(nst[:, t, :], x_sb[:, tiles[t], :])
                last.then_inc(norm_steps, 1)
                dve.wait_ge(norm_steps, 1)
                for t in range(BT):
                    last = v.bn_aggr(nmv[:, t, :], nst[:, t, :])
                last.then_inc(nstats_ready, 1)
                dve.wait_ge(norm_std, g + 1)
                v.reciprocal(nrs[:], nsd[:]).then_inc(norm_steps, 1)
                dve.wait_ge(norm_steps, 2)
                for t in range(BT):
                    last = v.tensor_scalar(n_sb[:, tiles[t], :], x_sb[:, tiles[t], :], nmv[:, t, 0:1],
                                           nrs[:, t:t + 1], ALU.subtract, ALU.mult)
                last.then_inc(n_ready, 1)

            def rank_tile(i, a):
                n = 0

                def after(instruction):
                    nonlocal n
                    n += 1
                    instruction.then_inc(rank_steps, 1)
                    dve.wait_ge(rank_steps, n)
                dve.sem_clear(rank_steps)
                dve.wait_ge(adj_in[a], i * 16 + 16)
                after(v.scalar_tensor_tensor(score[:], adj_sb[:, a, :], 0.0, pri[:],
                                             ALU.not_equal, ALU.mult))
                dve.sem_inc(adj_read, 1)
                for r in range(ROUNDS):
                    eight = top[:, a, r * TOP:(r + 1) * TOP]
                    after(v.max(eight, score[:]))
                    if r < ROUNDS - 1:
                        after(v.match_replace(score[:], eight, score[:], 0.0))
                v.tensor_scalar(nbr[:, a, :], top[:, a, 0:S], -1.0, none_row[:, bass.ds(i, 1)],
                                ALU.mult, ALU.add).then_inc(nbr_ready, 1)
                v.tensor_scalar(floor[:, a, :], top[:, a, S:S + 1], 0.5, LOWEST, ALU.is_gt, ALU.mult)

            def reduce_tile(i, a):
                dve.wait_ge(gathered[a], i * (16 * S) + 16 * S)
                v.tensor_reduce(agg[:, a, :], got[:, a, :, :].rearrange("p k c -> p c k"),
                                AX.X, ALU.max).then_inc(reduced, 1)
                dve.wait_ge(reduced, i * GT + (a + 1))
                v.tensor_scalar(agg[:, a, :], agg[:, a, :], floor[:, a, :], None,
                                ALU.max).then_inc(agg_ready, 1)

            def feed_forward(i):
                n = 0

                def after(instruction):
                    nonlocal n
                    n += 1
                    instruction.then_inc(ffn_steps, 1)
                    dve.wait_ge(ffn_steps, n)
                tiles = bass.ds(i * GT, GT)
                dve.sem_clear(ffn_steps)
                dve.wait_ge(lin_ready, i + 1)
                after(v.scalar_tensor_tensor(x1[:], lin[:], 0.0, x_sb[:, tiles, :], ALU.max, ALU.add))
                for a in range(GT):
                    ins = v.bn_stats(st[:, a, :], x1[:, a, :])
                after(ins)
                for a in range(GT):
                    ins = v.bn_aggr(mv[:, a, :], st[:, a, :])
                ins.then_inc(x1_stats, 1)
                dve.wait_ge(x1_std, i + 1)
                after(v.reciprocal(rs[:], sd[:]))
                for a in range(GT):
                    ins = v.tensor_scalar(m[:, a, :], x1[:, a, :], mv[:, a, 0:1], rs[:, a:a + 1],
                                          ALU.subtract, ALU.mult)
                ins.then_inc(m_ready, 1)
                v.tensor_tensor(xb[:], x1[:], beta_sb[:].unsqueeze(1).to_broadcast([P, GT, C]), ALU.add)

                dve.wait_ge(logit_ready, i + 1)
                after(v.tensor_copy(logit[:], gates_ps[:, 0:GT * E].rearrange("p (a e) -> p a e", a=GT)))
                for a in range(GT):
                    ins = v.max(top2[:, a, :], logit[:, a, :])
                after(ins)
                v.tensor_tensor(gap[:], top2[:, :, 1], top2[:, :, 0], ALU.subtract).then_inc(gap_ready, 1)
                for a in range(GT):
                    ins = v.max_index(pick[:, a, :], top2[:, a, :], logit[:, a, :])
                after(ins)
                v.tensor_copy(pickf[:], pick[:, :, 0:2])
                dve.wait_ge(exp_ready, i + 1)
                after(v.tensor_scalar(den[:], eg[:], 1.0, None, ALU.add))
                after(v.reciprocal(wa[:], den[:]))
                after(v.tensor_tensor(wb[:], eg[:], wa[:], ALU.mult))
                for a in range(GT):
                    v.tensor_scalar(ga[:, a, :], expert_ids, pickf[:, a, 0:1], wa[:, a:a + 1],
                                    ALU.is_equal, ALU.mult)
                    ins = v.tensor_scalar(gb2[:, a, :], expert_ids, pickf[:, a, 1:2], wb[:, a:a + 1],
                                          ALU.is_equal, ALU.mult)
                after(ins)
                v.tensor_tensor(gate[:], ga[:], gb2[:], ALU.add).then_inc(gate_ready, 1)

                dve.wait_ge(bias_ready, i + 1)
                after(v.tensor_tensor(y[:], turned_agg[:], m[:], ALU.add))
                for e in range(E):
                    dve.wait_ge(o_ready, i * E + (e + 1))
                    for a in range(GT):
                        ins = v.scalar_tensor_tensor(y[:, a, :], o_ps[e % 2][:, a, :], gate[:, a, e:e + 1],
                                                     y[:, a, :], ALU.mult, ALU.add)
                    ins.then_inc(o_used, 1)
                    dve.wait_ge(o_used, i * E + (e + 1))

                for a in range(GT):
                    ins = v.bn_stats(st2[:, a, :], y[:, a, :])
                after(ins)
                for a in range(GT):
                    ins = v.bn_aggr(mv2[:, a, :], st2[:, a, :])
                ins.then_inc(y_stats, 1)
                dve.wait_ge(y_std, i + 1)
                after(v.reciprocal(rs2[:], sd2[:]))
                for a in range(GT):
                    ins = v.tensor_scalar(z[:, a, :], y[:, a, :], mv2[:, a, 0:1], rs2[:, a:a + 1],
                                          ALU.subtract, ALU.mult)
                after(ins)
                after(v.tensor_tensor(z[:], z[:], gamma_sb[:].unsqueeze(1).to_broadcast([P, GT, C]), ALU.mult))
                dve.wait_ge(out_stored, i * 16 + 16)
                v.tensor_tensor(res[:], z[:], xb[:], ALU.add).then_inc(res_ready, 1)

            for a in range(GT):
                rank_tile(0, a)
            with dve.Fori(0, GROUPS - 1) as i:
                for a in range(GT):
                    reduce_tile(i, a)
                    rank_tile(i + 1, a)
                feed_forward(i)
            for a in range(GT):
                reduce_tile(GROUPS - 1, a)
            feed_forward(GROUPS - 1)

        @block.scalar
        def _(act):
            s = nc.scalar
            act.wait_ge(pool_ready, 3)
            with act.Fori(0, B) as g:
                act.wait_ge(nstats_ready, g + 1)
                s.activation(nsd[:], nmv[:, :, 1], ACT.Sqrt, bias=eps[:]).then_inc(norm_std, 1)
            act.wait_ge(consts_in, 16 * CONST_LOADS)
            act.wait_ge(n_ready, B)
            with act.Fori(0, GROUPS) as i:
                s.copy(n_grp[:], n_sb[:, bass.ds(i * GT, GT), :]).then_inc(n_taken, 1)
                act.wait_ge(nT_turned, i + 1)
                s.copy(nT[:], turned[:]).then_inc(nT_ready, 1)
                act.wait_ge(aggT_turned, i + 1)
                s.copy(aggT[:], turned_agg[:]).then_inc(aggT_ready, 1)
                act.wait_ge(x1_stats, i + 1)
                s.activation(sd[:], mv[:, :, 1], ACT.Sqrt, bias=eps[:]).then_inc(x1_std, 1)
                act.wait_ge(m_turned, i + 1)
                s.copy(mT[:], turned[:]).then_inc(mT_ready, 1)
                act.wait_ge(gap_ready, i + 1)
                s.activation(eg[:], gap[:], ACT.Exp).then_inc(exp_ready, 1)
                act.wait_ge(gate_turned, i + 1)
                s.copy(gateT[:], gates_ps[0:E, :].rearrange("e (a p) -> e a p", a=GT)).then_inc(gateT_ready, 1)
                for e in range(E):
                    for f in range(FC):
                        act.wait_ge(h_ready, i * (E * FC) + (e * FC + f + 1))
                        if e < 2:
                            pass
                        else:
                            act.wait_ge(o_ready, i * E + (e - 1))
                        s.activation(h_sb[:, e % 2, f, :], h_ps[f][:], ACT.Relu,
                                     bias=b1_sb[:, e, f:f + 1]).then_inc(relu_ready, 1)
                act.wait_ge(y_stats, i + 1)
                s.activation(sd2[:], mv2[:, :, 1], ACT.Sqrt, bias=eps[:]).then_inc(y_std, 1)

        @block.tensor
        def _(pe):
            t = nc.tensor
            pe.wait_ge(consts_in, 16 * CONST_LOADS)
            pe.wait_ge(pool_ready, 3)
            with pe.Fori(0, GROUPS) as i:
                pe.wait_ge(n_taken, i + 1)
                for a in range(GT):
                    ins = t.transpose(turned[:, a, :], n_grp[:, a, :], ident)
                ins.then_inc(nT_turned, 1)
                pe.wait_ge(agg_ready, i * GT + GT)
                for a in range(GT):
                    ins = t.transpose(turned_agg[:, a, :], agg[:, a, :], ident)
                ins.then_inc(aggT_turned, 1)
                pe.wait_ge(nT_ready, i + 1)
                pe.wait_ge(aggT_ready, i + 1)
                for a in range(GT):
                    t.matmul(lin[:, a, :], nT[:, a, :], W_sb[:, 0, :], start=True, stop=False)
                    t.matmul(lin[:, a, :], aggT[:, a, :], W_sb[:, 1, :], start=False, stop=False)
                    ins = t.matmul(lin[:, a, :], ones[:], rows[:, 0:C], start=False, stop=True)
                ins.then_inc(lin_ready, 1)
                pe.wait_ge(m_ready, i + 1)
                for a in range(GT):
                    ins = t.transpose(turned[:, a, :], m[:, a, :], ident)
                ins.then_inc(m_turned, 1)
                pe.wait_ge(mT_ready, i + 1)
                for a in range(GT):
                    t.matmul(gates_ps[:, a * E:(a + 1) * E], mT[:, a, :], gw_sb[:], start=True, stop=False)
                    ins = t.matmul(gates_ps[:, a * E:(a + 1) * E], ones[:], rows[:, C:C + E],
                                   start=False, stop=True)
                ins.then_inc(logit_ready, 1)

                def inner(e):
                    for f in range(FC):
                        if e >= 1:
                            pe.wait_ge(relu_ready, i * (E * FC) + ((e - 1) * FC + f + 1))
                        t.matmul(h_ps[f][:], w1_sb[:, e, f * P:(f + 1) * P], mT[:].rearrange("p a q -> p (a q)"),
                                 start=True, stop=True).then_inc(h_ready, 1)

                inner(0)
                pe.wait_ge(gate_ready, i + 1)
                for a in range(GT):
                    ins = t.transpose(gates_ps[0:E, a * P:(a + 1) * P], gate[:, a, :], ident)
                ins.then_inc(gate_turned, 1)
                pe.wait_ge(gateT_ready, i + 1)
                for a in range(GT):
                    ins = t.matmul(turned_agg[:, a, :], gateT[:, a, :], b2_sb[:], start=True, stop=True)
                ins.then_inc(bias_ready, 1)
                for e in range(E):
                    if e + 1 < E:
                        inner(e + 1)
                    pe.wait_ge(relu_ready, i * (E * FC) + (e + 1) * FC)
                    if e >= 2:
                        pe.wait_ge(o_used, i * E + (e - 1))
                    for a in range(GT):
                        for f in range(FC):
                            ins = t.matmul(o_ps[e % 2][:, a, :], h_sb[:, e % 2, f, a * P:(a + 1) * P],
                                           w2_sb[:, e, f, :], start=(f == 0), stop=(f == FC - 1))
                    ins.then_inc(o_ready, 1)


    return nc


INPUTS = ("x", "adj", "L0_gnn_W", "L0_gnn_b", "L0_ffn_gate_w", "L0_ffn_gate_b", "L0_ffn_w1", "L0_ffn_b1",
          "L0_ffn_w2", "L0_ffn_b2", "L0_ffn_gamma", "L0_ffn_beta")


def kernel(**inputs):
    import concourse.bacc as bacc
    from concourse.bass_utils import run_bass_kernel_spmd

    laid = {name: np.ascontiguousarray(inputs[name]) for name in INPUTS}
    laid["L0_ffn_b1"] = np.ascontiguousarray(laid["L0_ffn_b1"].reshape(E, FC, P).transpose(2, 0, 1))
    laid.update(shape_constants())

    nc = bacc.Bacc("TRN2", target_bir_lowering=False, num_devices=1)
    args = [nc.dram_tensor(f"in_{k}", v.shape, mybir.dt.from_np(v.dtype), kind="ExternalInput").ap()
            for k, v in laid.items()]
    out = nc.dram_tensor("out", (B, N, C), F32, kind="ExternalOutput").ap()
    build(nc, *args, out)
    r = run_bass_kernel_spmd(nc, [{f"in_{k}": v for k, v in laid.items()}], core_ids=[0])
    return r.results[0]["out"]
```

```python
from contextlib import ExitStack

import numpy as np

import concourse.bass as bass
from concourse import mybir

F32 = mybir.dt.float32
F16 = mybir.dt.float16
I32 = mybir.dt.int32
U32 = mybir.dt.uint32
ALU = mybir.AluOpType
ACT = mybir.ActivationFunctionType
AX = mybir.AxisListType

P = 128
B, N, C = 8, 1024, 128
S = 25
E, F = 16, 256
FC = F // P
TILES = B * N // P
GT = 4
GROUPS = TILES // GT
GN = GT * P
BT = N // P
GB = BT // GT
ROWS = N + 1
EPS = 1e-5
LOWEST = -3.0e38
TOP = 8
ROUNDS = -(-(S + 1) // TOP)

RUNS = N // P
R, L = 5, 5
HIT = 64.0
DROP = 64.0
SCALE = 1024.0
PERIODS = R
PU = RUNS // 2 + 1
MIDDLE = PU // 2
UNITS = PERIODS * PU
MASKS = 2 * PERIODS
RING = 3
BANKS = [u % RING for u in range(UNITS - 1)] + [(UNITS - 1) % RING if (UNITS - 1) % RING else 1]
MASK_RING = 5
assert R == L and MASKS % MASK_RING == 0 and RUNS % 2 == 0 and S < HIT


def shape_constants():
    first = np.zeros((P, 2 * P), np.float32)
    first[:, :P] = np.eye(P)
    first[:, P:P + E] = np.arange(E)
    first[:, P + E:P + E + TILES] = (np.arange(TILES) // BT) * ROWS + N
    priority = np.broadcast_to((N - np.arange(N)).astype(np.float16), (P, N))
    count = np.triu(np.ones((P, P)))
    counting = np.stack([count, count + HIT * np.eye(P), np.ones((P, P)), -DROP * np.eye(P)], 1)
    return {"small": first, "priority": np.ascontiguousarray(priority),
            "counting": counting.astype(np.float16)}


HALVES = 2
TR = HALVES * P
QUEUE = B * N + TR
MOE_TILES = 2 * B * N // TR + E
ROW_TILES = E * QUEUE // TR + 1
SLOTS = 4
AHEAD = 3
GB2 = 2
GRID_COLS = GT * E + MOE_TILES
assert QUEUE % TR == 0 and MOE_TILES % SLOTS == 0 and TR == 1 << (TR.bit_length() - 1)


def moe_constants():
    start = np.arange(E) * QUEUE
    grid = np.zeros((P, GRID_COLS), np.float32)
    grid[:, 0:GT * E] = np.tile(start, GT)
    grid[:, GT * E:] = np.arange(MOE_TILES)
    before = np.stack([np.triu(np.ones((P, P)), 1), np.ones((P, P))], 1)
    return {"moe_small": grid, "gate_consts": before.astype(np.float16)}


def ranking_items():
    order = [("all", 0)]
    for b in range(1, RUNS):
        order += [("all", b), ("run", b - 1)]
    order += [("run", RUNS - 1), ("degree", 0)]
    order += [("rest", b) for b in range(RUNS)] + [("rest_count", 0)]
    bank = {"all": lambda b: 0, "run": lambda b: 1, "degree": lambda b: 0,
            "rest": lambda b: (b + 1) % 2, "rest_count": lambda b: 1}
    return [(kind, b, bank[kind](b)) for kind, b in order]


ITEMS = ranking_items()
AT = {(kind, b): n for n, (kind, b, _) in enumerate(ITEMS)}
BEHIND = {}
for _kind, _b, _ in ITEMS:
    BEHIND[_kind, _b] = {"all": _b, "run": _b + 1, "degree": RUNS + 1, "rest": RUNS + 4 + _b,
                         "rest_count": 2 * RUNS + 4}[_kind]
assert max(BEHIND.values()) <= UNITS - PU


def build(nc, x, adj, adj_t, W, b, gate_w, gate_b, w1, b1, w2, b2, gamma, beta, small, priority, counting,
          moe_small, gate_consts, out):
    with ExitStack() as ctx:
        def sb(name, shape, dt=F32):
            return ctx.enter_context(nc.sbuf_tensor(name, shape, dt))

        const = sb("const", [P, 2 * P])
        eps = sb("eps", [P, 1])
        x_sb = sb("x_sb", [P, TILES, C])
        mean_sb = sb("mean_sb", [P, TILES, 2])
        rstd = sb("rstd", [P, TILES])
        flag = sb("flag", [P, 1], I32)
        weight_all = sb("weight_all", [P, 2, TILES])
        slot_all = sb("slot_all", [P, 2 * TILES], I32)
        tile_row = sb("tile_row", [1, MOE_TILES], I32)
        tile_expert = sb("tile_expert", [1, MOE_TILES], I32)
        rows_in = nc.dram_tensor("rows_in", (ROW_TILES * TR, C), F32).ap()
        rows_out = nc.dram_tensor("rows_out", (MOE_TILES * TR, C), F32).ap()
        agg_T = sb("agg_T", [P, TILES * P])
        neighbour_maxima(nc, x, adj_t, small, counting, const, eps, x_sb, mean_sb, rstd, agg_T, flag)
        general_maxima(nc, adj, priority, const, x_sb, mean_sb, rstd, agg_T, flag)
        m_all = sb("m_all", [P, TILES, C])
        w1_sb = sb("w1_sb", [P, E, F])
        w2_sb = sb("w2_sb", [P, E, FC * C])
        b1_sb = sb("b1_sb", [P, E, F])
        b2_sb = sb("b2_sb", [P, E, C])
        expert_loads = (
            (w1_sb[:], w1.rearrange("e p f -> p e f")),
            (b1_sb[:].rearrange("p e f -> p (e f)"), b1.rearrange("e f -> (e f)").partition_broadcast(P)),
            (w2_sb[:].rearrange("p e (k c) -> p e k c", k=FC), w2.rearrange("e (k p) c -> p e k c", p=P)),
            (b2_sb[:].rearrange("p e c -> p (e c)"), b2.rearrange("e c -> (e c)").partition_broadcast(P)),
        )
        tokens(nc, W, b, gate_w, gate_b, moe_small, gate_consts, x_sb, mean_sb, rstd, agg_T, m_all,
               weight_all, slot_all, tile_row, tile_expert, rows_in, const, eps, expert_loads)
        experts(nc, w1_sb, b1_sb, w2_sb, b2_sb, const, tile_row, tile_expert, rows_in, rows_out)
        results(nc, gamma, beta, out, x_sb, m_all, weight_all, slot_all, rows_out, eps)
    return nc


def neighbour_maxima(nc, x, adj_t, small, counting, const, eps, x_sb, mean_sb, rstd, agg_T, flag):
    with ExitStack() as ctx:
        def sb(name, shape, dt=F32):
            return ctx.enter_context(nc.sbuf_tensor(name, shape, dt))

        def ps(name, shape):
            return ctx.enter_context(nc.psum_tensor(name, shape, F32))

        def sem(name):
            return ctx.enter_context(nc.semaphore(name))

        cnt = sb("cnt", [P, 4, P], F16)
        COUNT, CODE, ALL, LESS = (cnt[:, k, :] for k in range(4))
        beyond_s = sb("beyond_s", [P, 1])
        beyond_l = sb("beyond_l", [P, 1])
        ones_f = sb("ones_f", [P, P])
        nst = sb("nst", [P, BT, 6])
        nmv = sb("nmv", [P, BT, 2])
        std = sb("std", [P, TILES])
        n_scale = sb("n_scale", [P, TILES])
        n_shift = sb("n_shift", [P, TILES])
        n_next = sb("n_next", [P, BT, C])
        hi_next = sb("hi_next", [P, BT, C], F16)
        lo_next = sb("lo_next", [P, BT, C], F16)
        hi = sb("hi", [P, BT, C], F16)
        lo = sb("lo", [P, BT, C], F16)
        adj_sb = sb("adj_sb", [P, RUNS, GN], I32)
        edge = sb("edge", [P, RUNS, GN], F16)
        run_sum = sb("run_sum", [P, RUNS - 1, GN], F16)
        over = sb("over", [P, 2, GN], F16)
        code = sb("code", [P, 2, RUNS, GN], F16)
        rest = sb("rest", [P, RUNS, GN], F16)
        rest_code = sb("rest_code", [P, 2, RUNS, GN], F16)
        many = sb("many", [P, 2, GN], F16)
        mask = sb("mask", [P, MASK_RING, RUNS, GN], F16)
        best = sb("best", [P, 2, 2, GN])
        junk = sb("junk", [P, GN], F16)
        zero_flag = sb("zero_flag", [P, GROUPS])
        rest_flag = sb("rest_flag", [P, GROUPS])
        flags = sb("flags", [P, 2])

        rank_ps = [ps(f"rank_ps{k}", [P, GN]) for k in range(2)]
        unit_ps = [ps(f"unit_ps{k}", [P, 2, GN]) for k in range(RING)]

        small_in = sem("small_in")
        cnt_in = sem("cnt_in")
        x_in = sem("x_in")
        adj_in = sem("adj_in")
        pool_ready = sem("pool_ready")
        stat_steps = sem("stat_steps")
        var_ready = sem("var_ready")
        std_ready = sem("std_ready")
        scale_ready = sem("scale_ready")
        next_ready = sem("next_ready")
        next_steps = sem("next_steps")
        lo_ready = sem("lo_ready")
        parts_ready = sem("parts_ready")
        edge_ready = sem("edge_ready")
        edge_summed = sem("edge_summed")
        rest_ready = sem("rest_ready")
        rest_summed = sem("rest_summed")
        item_done = sem("item_done")
        item_read = sem("item_read")
        mask_ready = sem("mask_ready")
        unit_done = sem("unit_done")
        first_max = sem("first_max")
        unit_used = sem("unit_used")
        best_free = sem("best_free")
        best_merged = sem("best_merged")
        agg_ready = sem("agg_ready")
        flag_steps = sem("flag_steps")
        flags_summed = sem("flags_summed")

        NI = len(ITEMS)
        x_t = x.rearrange("b (t p) c -> p (b t) c", p=P)
        adj_g = adj_t.rearrange("q (k p) i -> q p k i", p=P)
        block = ctx.enter_context(nc.Block())

        @block.sync
        def _(sp):
            sp.dma_start(adj_sb[:], adj_g[0]).then_inc(adj_in, 16)
            sp.dma_start(cnt[:], counting).then_inc(cnt_in, 16)
            sp.dma_start(const[:], small).then_inc(small_in, 16)
            for k in range(4):
                tiles = slice(k * TILES // 4, (k + 1) * TILES // 4)
                sp.dma_start(x_sb[:, tiles, :], x_t[:, tiles, :]).then_inc(x_in, 16)
            with sp.Fori(0, GROUPS - 1) as q:
                sp.wait_ge(edge_ready, q + 1)
                sp.dma_start(adj_sb[:], adj_g[q + 1]).then_inc(adj_in, 16)

        @block.gpsimd
        def _(pool):
            g = nc.gpsimd
            g.memset(eps[:], EPS).then_inc(pool_ready, 1)
            g.memset(beyond_s[:], -float(S)).then_inc(pool_ready, 1)
            g.memset(beyond_l[:], -float(L)).then_inc(pool_ready, 1)
            g.memset(ones_f[:], 1.0).then_inc(pool_ready, 1)

            def sums(q, src, ready, summed):
                dst = run_sum
                pool.wait_ge(ready, q + 1)
                for b in range(2, RUNS + 1):
                    if b > 2:
                        pool.wait_ge(summed, q * (RUNS - 1) + (b - 2))
                    before = src[:, 0, :] if b == 2 else dst[:, b - 3, :]
                    g.tensor_tensor(dst[:, b - 2, :], before, src[:, b - 1, :], ALU.add).then_inc(summed, 1)

            def low_part(gr):
                pool.wait_ge(next_ready, gr + 1)
                g.tensor_tensor(lo_next[:], n_next[:], hi_next[:], ALU.subtract).then_inc(lo_ready, 1)

            def prepare(q):
                sums(q, edge, edge_ready, edge_summed)
                pool.wait_ge(item_done, q * NI + (AT["degree", 0] + 1))
                sums(q, rest, rest_ready, rest_summed)

            low_part(0)
            prepare(0)
            with pool.Fori(0, B - 1) as gr:
                prepare(gr * GB + 1)
                low_part(gr + 1)
                prepare(gr * GB + 2)
            prepare((B - 1) * GB + 1)

        def rank_item(pe, q, n):
            kind, b, bank = ITEMS[n]
            t = nc.tensor
            before_q = q - 1
            dst = rank_ps[bank][:]
            earlier = [k for k in range(n) if ITEMS[k][2] == bank]
            if earlier:
                pe.wait_ge(item_read, q * NI + (earlier[-1] + 1))
            elif not (isinstance(q, int) and q == 0):
                last = max(k for k in range(NI) if ITEMS[k][2] == bank)
                pe.wait_ge(item_read, q * NI + (last + 1 - NI))
            if kind == "all":
                if b == 0:
                    pe.wait_ge(edge_ready, q + 1)
                if b >= 2:
                    pe.wait_ge(edge_summed, q * (RUNS - 1) + (b - 1))
                ins = t.matmul(dst, COUNT, edge[:, b, :], start=True, stop=(b == 0))
                if b > 0:
                    ins = t.matmul(dst, ALL, edge[:, 0, :] if b == 1 else run_sum[:, b - 2, :],
                                   start=False, stop=True)
            elif kind == "run":
                t.matmul(dst, CODE, edge[:, b, :], start=True, stop=False)
                pe.wait_ge(item_read, q * NI + (AT["all", b] + 1))
                ins = t.matmul(dst, LESS, over[:, b % 2, :], start=False, stop=True)
            elif kind == "degree":
                pe.wait_ge(edge_summed, q * (RUNS - 1) + (RUNS - 1))
                ins = t.matmul(dst, ALL, run_sum[:, RUNS - 2, :], start=True, stop=True)
            elif kind == "rest":
                if b == 0:
                    pe.wait_ge(rest_ready, q + 1)
                if b >= 2:
                    pe.wait_ge(rest_summed, q * (RUNS - 1) + (b - 1))
                ins = t.matmul(dst, CODE, rest[:, b, :], start=True, stop=(b == 0))
                if b > 0:
                    ins = t.matmul(dst, ALL, rest[:, 0, :] if b == 1 else run_sum[:, b - 2, :],
                                   start=False, stop=True)
            else:
                pe.wait_ge(rest_summed, q * (RUNS - 1) + (RUNS - 1))
                ins = t.matmul(dst, ALL, run_sum[:, RUNS - 2, :], start=True, stop=True)
            ins.then_inc(item_done, 1)

        def slots_of(u):
            period, k = divmod(u, PU)
            if k == MIDDLE:
                return [(2 * period + 1, list(range(RUNS)))]
            b = 2 * (k if k < MIDDLE else k - 1)
            return [(2 * period, [b]), (2 * period, [b + 1])]

        def last_unit(k):
            return max(u for u in range(UNITS) if any(c == k for c, _ in slots_of(u)))

        @block.tensor
        def _(pe):
            t = nc.tensor
            pe.sem_inc(unit_done, UNITS)
            pe.wait_ge(cnt_in, 16)
            pe.wait_ge(pool_ready, 4)
            for n in range(NI):
                rank_item(pe, 0, n)

            def unit(q, gr, h, u):
                if u == 0 and h == 0:
                    pe.wait_ge(parts_ready, 2 * gr + 1)
                if u == MIDDLE and h == 0:
                    pe.wait_ge(parts_ready, 2 * gr + 2)
                same = [k for k in range(UNITS) if BANKS[k] == BANKS[u]]
                before = max(k + UNITS if k < u else k for k in same if k != u)
                pe.wait_ge(unit_used, q * UNITS + (before + 1))
                for s, (k, runs) in enumerate(slots_of(u)):
                    pe.wait_ge(mask_ready, q * MASKS + (k + 1))
                    for b in runs:
                        m = mask[:, k % MASK_RING, b, :]
                        dst = unit_ps[BANKS[u]][:, s, :]
                        t.matmul(dst, hi[:, b, :], m, start=(b == runs[0]), stop=False)
                        ins = t.matmul(dst, lo[:, b, :], m, start=False, stop=(b == runs[-1]))
                ins.then_inc(unit_done, 1)

            def group(q, gr, h, more):
                for u in range(UNITS):
                    unit(q, gr, h, u)
                    if more:
                        for n, (kind, b, _) in enumerate(ITEMS):
                            if BEHIND[kind, b] == u:
                                rank_item(pe, q + 1, n)

            with pe.Fori(0, B - 1) as gr:
                for h in range(GB):
                    group(gr * GB + h, gr, h, True)
            for h in range(GB):
                group((B - 1) * GB + h, B - 1, h, h == 0)
            pe.wait_ge(flag_steps, 2)
            t.matmul(rank_ps[0][:, 0:1], ones_f[:], flags[:, 0:1], start=True, stop=True).then_inc(flags_summed, 1)

        @block.scalar
        def _(act):
            s = nc.scalar
            act.wait_ge(pool_ready, 4)

            def item(q, h, n):
                kind, b, bank = ITEMS[n]
                src = rank_ps[bank][:]
                act.wait_ge(item_done, q * NI + (n + 1))
                if kind == "all":
                    ins = s.activation(over[:, b % 2, :], src, ACT.Relu, bias=beyond_s[:])
                elif kind == "run":
                    ins = s.copy(code[:, h, b, :], src)
                elif kind == "degree":
                    ins = s.activation(many[:, h, :], src, ACT.Relu, bias=beyond_s[:])
                elif kind == "rest":
                    ins = s.copy(rest_code[:, h, b, :], src)
                else:
                    column = slice(0, 1) if isinstance(q, int) and q == 0 else bass.ds(q, 1)
                    ins = s.activation(src, src, ACT.Relu, bias=beyond_l[:],
                                       accum_out=rest_flag[:, column])
                ins.then_inc(item_read, 1)

            def parts(gr):
                if not isinstance(gr, int):
                    act.wait_ge(parts_ready, 2 * gr)
                for t in range(BT):
                    col = bass.ds(gr * BT + t, 1)
                    ins = s.activation(n_next[:, t, :], x_sb[:, col, :], ACT.Identity,
                                       bias=n_shift[:, col], scale=n_scale[:, col])
                ins.then_inc(next_steps, 1)
                act.wait_ge(next_steps, gr + 1)
                s.copy(hi_next[:], n_next[:]).then_inc(next_ready, 1)

            def group(q, gr, h, more):
                ahead = [n for n, (kind, b, _) in enumerate(ITEMS) if BEHIND[kind, b] <= 1]
                if more:
                    for n in ahead:
                        item(q + 1, (h + 1) % 2, n)
                act.wait_ge(best_free, q + 1)
                act.wait_ge(unit_done, q * UNITS + (UNITS + 1))
                s.copy(best[:, 0, :, :], unit_ps[0][:]).then_inc(first_max, 1)
                if more:
                    for n in range(len(ahead), NI):
                        item(q + 1, (h + 1) % 2, n)

            act.wait_ge(var_ready, 1)
            s.activation(std[:], mean_sb[:, :, 1], ACT.Sqrt, bias=eps[:]).then_inc(std_ready, 1)
            act.wait_ge(scale_ready, 1)
            parts(0)
            for n in range(NI):
                item(0, 0, n)
            with act.Fori(0, B - 1) as gr:
                group(gr * GB, gr, 0, True)
                parts(gr + 1)
                group(gr * GB + 1, gr, 1, True)
            group((B - 1) * GB, B - 1, 0, True)
            group((B - 1) * GB + 1, B - 1, 1, False)

        @block.vector
        def _(dve):
            v = nc.vector

            def edges(q):
                dve.wait_ge(adj_in, q * 16 + 16)
                v.tensor_scalar(edge[:], adj_sb[:], 0.0, None, ALU.not_equal).then_inc(edge_ready, 1)

            def rests(q, h):
                dve.wait_ge(item_read, q * NI + (AT["run", RUNS - 1] + 1))
                v.tensor_scalar(rest[:], code[:, h, :, :], HIT + R + 0.5, None,
                                ALU.is_gt).then_inc(rest_ready, 1)

            dve.wait_ge(x_in, 4 * 16)
            edges(0)
            with dve.Fori(0, B) as g:
                dve.sem_clear(stat_steps)
                for t in range(BT):
                    ins = v.bn_stats(nst[:, t, :], x_sb[:, bass.ds(g * BT + t, 1), :])
                ins.then_inc(stat_steps, 1)
                dve.wait_ge(stat_steps, 1)
                for t in range(BT):
                    ins = v.bn_aggr(nmv[:, t, :], nst[:, t, :])
                ins.then_inc(stat_steps, 1)
                dve.wait_ge(stat_steps, 2)
                ins = v.tensor_copy(mean_sb[:, bass.ds(g * BT, BT), :], nmv[:])
                ins.then_inc(stat_steps, 1)
                dve.wait_ge(stat_steps, 3)
            v.engine_nop().then_inc(var_ready, 1)
            dve.wait_ge(std_ready, 1)
            v.reciprocal(rstd[:], std[:]).then_inc(stat_steps, 1)
            dve.wait_ge(stat_steps, 4)
            v.tensor_scalar(n_scale[:], rstd[:], SCALE, None, ALU.mult).then_inc(stat_steps, 1)
            dve.wait_ge(stat_steps, 5)
            v.scalar_tensor_tensor(n_shift[:], mean_sb[:, :, 0], -1.0, n_scale[:], ALU.mult,
                                   ALU.mult).then_inc(scale_ready, 1)
            rests(0, 0)

            dve.sem_inc(unit_used, UNITS)
            dve.sem_inc(best_free, 1)

            def take_parts(runs):
                v.tensor_copy(hi[:, runs, :], hi_next[:, runs, :])
                v.tensor_copy(lo[:, runs, :], lo_next[:, runs, :]).then_inc(parts_ready, 1)

            def build_mask(q, h, k):
                old = k - MASK_RING
                if old >= 0:
                    dve.wait_ge(unit_done, q * UNITS + (UNITS + last_unit(old) + 1))
                else:
                    dve.wait_ge(unit_done, q * UNITS + (last_unit(old + MASKS) + 1))
                src, rank = (rest_code if k % 2 else code), k // 2 + 1
                if k == 0:
                    dve.wait_ge(item_read, q * NI + (AT["run", RUNS - 1] + 1))
                if k == 1:
                    dve.wait_ge(item_read, q * NI + NI)
                v.tensor_scalar(mask[:, k % MASK_RING, :, :], src[:, h, :, :], HIT + rank, None,
                                ALU.is_equal).then_inc(mask_ready, 1)

            def use(q, u):
                if u == 0:
                    dve.wait_ge(first_max, q + 1)
                    dve.sem_inc(unit_used, 1)
                    return
                dve.wait_ge(unit_done, q * UNITS + (UNITS + u + 1))
                if u == 1:
                    v.tensor_copy(best[:, 1, :, :], unit_ps[BANKS[u]][:]).then_inc(unit_used, 1)
                    return
                dve.wait_ge(unit_used, q * UNITS + (UNITS + u - 1))
                n = len(slots_of(u))
                mine = best[:, u % 2, 0:n, :]
                v.tensor_tensor(mine, unit_ps[BANKS[u]][:, 0:n, :], mine, ALU.max).then_inc(unit_used, 1)

            def group(q, gr, h, more, edges_too, next_graph):
                for u in range(UNITS):
                    period, k = divmod(u, PU)
                    if more and u == RUNS + 2:
                        rests(q + 1, (h + 1) % 2)
                    if k == MIDDLE and period < PERIODS - 1:
                        build_mask(q, h, 2 * period + 2)
                        build_mask(q, h, 2 * period + 3)
                    if k == MIDDLE and period == PERIODS - 1 and more:
                        build_mask(q + 1, (h + 1) % 2, 0)
                        build_mask(q + 1, (h + 1) % 2, 1)
                    if edges_too and u == UNITS - PU + 1:
                        dve.wait_ge(item_done, q * NI + 2 * NI)
                        edges(q + 2)
                    if next_graph and u == UNITS - 1:
                        dve.wait_ge(lo_ready, gr + 2)
                        dve.wait_ge(unit_done, q * UNITS + (UNITS + (UNITS - PU + MIDDLE) + 1))
                        take_parts(slice(0, RUNS // 2))
                    use(q, u)
                if next_graph:
                    take_parts(slice(RUNS // 2, RUNS))
                dve.wait_ge(unit_used, q * UNITS + 2 * UNITS)
                columns = bass.ds(q * GN, GN)
                v.tensor_tensor(best[:, 0, :, :], best[:, 0, :, :], best[:, 1, :, :],
                                ALU.max).then_inc(best_merged, 1)
                dve.wait_ge(best_merged, q + 1)
                v.tensor_tensor(agg_T[:, columns], best[:, 0, 0, :], best[:, 0, 1, :],
                                ALU.max).then_inc(agg_ready, 1)
                dve.wait_ge(agg_ready, q + 1)
                dve.sem_inc(best_free, 1)
                v.scalar_tensor_tensor(junk[:], agg_T[:, columns], 0.0, many[:, h, :], ALU.is_equal,
                                       ALU.mult, accum_out=zero_flag[:, bass.ds(q, 1)])

            dve.wait_ge(lo_ready, 1)
            take_parts(slice(0, RUNS // 2))
            take_parts(slice(RUNS // 2, RUNS))
            build_mask(0, 0, 0)
            build_mask(0, 0, 1)
            dve.wait_ge(item_done, NI)
            edges(1)
            with dve.Fori(0, B - 1) as gr:
                group(gr * GB, gr, 0, True, True, False)
                group(gr * GB + 1, gr, 1, True, True, True)
            group((B - 1) * GB, B - 1, 0, True, False, False)
            group((B - 1) * GB + 1, B - 1, 1, False, False, False)
            dve.drain()
            dve.wait_ge(item_read, GROUPS * NI)
            v.tensor_tensor(zero_flag[:], zero_flag[:], rest_flag[:], ALU.add).then_inc(flag_steps, 1)
            dve.wait_ge(flag_steps, 1)
            v.reduce_max(flags[:, 0:1], zero_flag[:], AX.X).then_inc(flag_steps, 1)
            dve.wait_ge(flags_summed, 1)
            v.tensor_scalar(flag[:], rank_ps[0][:, 0:1], 0.5, None, ALU.is_gt)


def general_maxima(nc, adj, priority, const, x_sb, mean_sb, rstd, agg_T, flag):
    with ExitStack() as ctx:
        def sb(name, shape, dt=F32):
            return ctx.enter_context(nc.sbuf_tensor(name, shape, dt))

        def sem(name):
            return ctx.enter_context(nc.semaphore(name))

        ident = const[:, 0:P]
        none_row = const[:, P + E:P + E + TILES]
        table = nc.dram_tensor("gather_table", (B, ROWS, C), F32).ap()
        table_b = table[:, 0:N, :].rearrange("b (t p) c -> b t p c", p=P)
        table_rows = table.rearrange("b r c -> (b r) c")
        adj_tiles = adj.rearrange("b (t p) j -> (b t) p j", p=P)

        pri = sb("pri", [P, N], F16)
        zrow = sb("zrow", [B, C])
        n_tile = sb("n_tile", [P, C])
        adj_tile = sb("adj_tile", [P, N], I32)
        score = sb("score", [P, N], F16)
        top = sb("top", [P, ROUNDS * TOP])
        nbr = sb("nbr", [P, S], I32)
        floor = sb("floor", [P, 1])
        got = sb("got", [P, S, C])
        most = sb("most", [P, C])
        tile_agg = sb("tile_agg", [P, C])
        turned = ctx.enter_context(nc.psum_tensor("gen_turned", [P, P], F32))

        pri_in = sem("pri_in")
        zero_made = sem("zero_made")
        table_out = sem("gen_table_out")
        n_made = sem("n_made")
        n_stored = sem("n_stored")
        tile_in = sem("tile_in")
        rank_steps = sem("gen_rank_steps")
        nbr_ready = sem("gen_nbr_ready")
        begun = sem("gen_begun")
        gathered = sem("gen_gathered")
        tile_ready = sem("tile_ready")
        tile_turned = sem("tile_turned")
        tile_done = sem("tile_done")
        block = ctx.enter_context(nc.Block())

        @block.sync
        def _(sp):
            wanted = sp.value_load(flag[0:1, 0:1], min_val=0, max_val=1)
            with sp.If(wanted > 0):
                sp.dma_start(pri[:], priority).then_inc(pri_in, 16)
                sp.wait_ge(zero_made, 1)
                sp.dma_start(table[:, N, :], zrow[:]).then_inc(table_out, 16)
                with sp.Fori(0, B) as g:
                    for t in range(BT):
                        sp.wait_ge(n_made, g * BT + (t + 1))
                        sp.dma_start(table_b[g, t], n_tile[:]).then_inc(n_stored, 16)
                sp.wait_ge(n_stored, 16 * (TILES + 1))
                sp.wait_ge(table_out, 16)
                sp.sem_inc(table_out, 1)
                sp.dma_start(adj_tile[:], adj_tiles[0]).then_inc(tile_in, 16)
                with sp.Fori(0, TILES - 1) as t:
                    sp.wait_ge(tile_done, t + 1)
                    sp.dma_start(adj_tile[:], adj_tiles[t + 1]).then_inc(tile_in, 16)

        @block.gpsimd
        def _(pool):
            wanted = pool.value_load(flag[0:1, 0:1], min_val=0, max_val=1)
            with pool.If(wanted > 0):
                pool.memset(zrow[:], 0.0).then_inc(zero_made, 1)
                pool.wait_ge(table_out, 17)
                with pool.Fori(0, TILES) as t:
                    pool.wait_ge(nbr_ready, t + 1)
                    pool.sem_inc(begun, 1)
                    for k in range(S):
                        pool.indirect_dma_start(
                            out=got[:, k, :], out_offset=None, in_=table_rows,
                            in_offset=bass.IndirectOffsetOnAxis(ap=nbr[:, k:k + 1], axis=0),
                        ).then_inc(gathered, 16)

        @block.tensor
        def _(pe):
            wanted = pe.value_load(flag[0:1, 0:1], min_val=0, max_val=1)
            with pe.If(wanted > 0):
                with pe.Fori(0, TILES) as t:
                    pe.wait_ge(tile_ready, t + 1)
                    nc.tensor.transpose(turned[:], tile_agg[:], ident).then_inc(tile_turned, 1)

        @block.vector
        def _(dve):
            v = nc.vector
            wanted = dve.value_load(flag[0:1, 0:1], min_val=0, max_val=1)
            with dve.If(wanted > 0):
                dve.sem_inc(n_stored, 16)
                with dve.Fori(0, TILES) as t:
                    tile = bass.ds(t, 1)
                    dve.wait_ge(n_stored, t * 16 + 16)
                    v.tensor_scalar(n_tile[:], x_sb[:, tile, :].rearrange("p a c -> p (a c)"),
                                    mean_sb[:, tile, 0], rstd[:, tile], ALU.subtract,
                                    ALU.mult).then_inc(n_made, 1)
                dve.wait_ge(pri_in, 16)
                with dve.Fori(0, TILES) as t:
                    steps = [0]

                    def after(instruction):
                        steps[0] += 1
                        instruction.then_inc(rank_steps, 1)
                        dve.wait_ge(rank_steps, steps[0])
                    dve.sem_clear(rank_steps)
                    dve.wait_ge(tile_in, t * 16 + 16)
                    after(v.scalar_tensor_tensor(score[:], adj_tile[:], 0.0, pri[:], ALU.not_equal, ALU.mult))
                    for r in range(ROUNDS):
                        eight = top[:, r * TOP:(r + 1) * TOP]
                        after(v.max(eight, score[:]))
                        if r < ROUNDS - 1:
                            after(v.match_replace(score[:], eight, score[:], 0.0))
                    v.tensor_scalar(nbr[:], top[:, 0:S], -1.0, none_row[:, bass.ds(t, 1)],
                                    ALU.mult, ALU.add).then_inc(nbr_ready, 1)
                    after(v.tensor_scalar(floor[:], top[:, S:S + 1], 0.5, LOWEST, ALU.is_gt, ALU.mult))
                    dve.wait_ge(gathered, t * (16 * S) + 16 * S)
                    after(v.tensor_reduce(most[:], got[:].rearrange("p k c -> p c k"), AX.X, ALU.max))
                    after(v.tensor_scalar(most[:], most[:], floor[:], None, ALU.max))
                    v.tensor_scalar(tile_agg[:], most[:], SCALE, None, ALU.mult).then_inc(tile_ready, 1)
                    dve.wait_ge(tile_turned, t + 1)
                    v.tensor_copy(agg_T[:, bass.ds(t * P, P)], turned[:]).then_inc(tile_done, 1)
                    dve.wait_ge(tile_done, t + 1)


def tokens(nc, W, b, gate_w, gate_b, moe_small, gate_consts, x_sb, mean_sb, rstd, agg_T, m_all,
           weight_all, slot_all, tile_row, tile_expert, rows_in, const, eps, expert_loads):
    with ExitStack() as ctx:
        def sb(name, shape, dt=F32):
            return ctx.enter_context(nc.sbuf_tensor(name, shape, dt))

        def ps(name, shape, dt=F32):
            return ctx.enter_context(nc.psum_tensor(name, shape, dt))

        def sem(name):
            return ctx.enter_context(nc.semaphore(name))

        ident = const[:, 0:P]
        expert_ids = const[:, P:P + E]
        W_sb = sb("W_sb", [P, 2, C])
        rows = sb("rows", [1, C + E])
        ones = sb("ones", [1, P])
        gw_sb = sb("gw_sb", [P, E])
        grid = sb("grid", [P, GRID_COLS])
        earlier = sb("earlier", [P, 2, P], F16)
        EARLIER, ALL = earlier[:, 0, :], earlier[:, 1, :]
        queue_start = grid[:, 0:GT * E].rearrange("p (a e) -> p a e", a=GT)
        number = grid[0:1, GT * E:]
        zeros = sb("zeros", [P, HALVES * C])

        n_grp = sb("n_grp", [P, 2, GT, C])
        nT = sb("nT", [P, 2, GT, P])
        aggT = sb("aggT", [P, 2, GT, P])
        st = sb("st", [P, GT, 6])
        mv = sb("mv", [P, 2, GT, 2])
        sd = sb("sd", [P, 2, GT])
        rs = sb("rs", [P, GT])
        m = sb("m", [P, 2, GT, C])
        mT = sb("mT", [P, 2, GT, P])
        logit = sb("logit", [P, GT, E])
        top2 = sb("top2", [P, 2, GT, TOP])
        pick = sb("pick", [P, GT, TOP], U32)
        pickf = sb("pickf", [P, 2, GT])
        gap = sb("gap", [P, TILES])
        eg = sb("eg", [P, TILES])
        den = sb("den", [P, TILES])
        send = sb("send", [P, 2, GT, C])
        chosen = sb("chosen", [P, 2 * TILES, E], F16)
        place_all = sb("place_all", [P, 2 * TILES])
        both = sb("both", [P, 2, GT, E], F16)
        group_sum = sb("group_sum", [P, E], F16)
        run = sb("run", [P, GROUPS + 1, E], F16)
        place = sb("place", [P, GT, E])
        picked = sb("picked", [P, 2, GT, E])
        slot = sb("slot", [P, 2, 2 * GT], I32)
        count = sb("count", [P, E])
        tail = sb("tail", [1, E], I32)
        row = {k: sb(f"row_{k}", [P, E]) for k in ("tiles", "ones", "upto", "moved")}
        row_int = sb("row_int", [P, E], I32)
        moved = sb("moved", [P, 2 * TILES, E])
        past = sb("past", [1, MOE_TILES, E])
        line = {k: sb(f"line_{k}", [1, MOE_TILES]) for k in ("expert", "before", "index", "row")}
        move = sb("move", [P, 2 * TILES])

        turned = ps("turned", [P, GT, P])
        lin = [ps(f"lin{k}", [P, GT, C]) for k in range(2)]
        m_turned_ps = ps("m_turned_ps", [P, GT, P])
        logit_ps = [ps(f"logit_ps{k}", [P, GT, E]) for k in range(2)]
        place_ps = [ps(f"place_ps{k}", [P, GT, E]) for k in range(2)]

        consts_in = sem("consts_in")
        pool_ready = sem("tok_pool_ready")
        spare_out = sem("spare_out")
        weights_in = sem("weights_in")
        n_taken = sem("n_taken")
        nT_turned = sem("nT_turned")
        nT_ready = sem("nT_ready")
        aggT_ready = sem("aggT_ready")
        lin_ready = sem("lin_ready")
        x1_steps = sem("x1_steps")
        x1_stats = sem("x1_stats")
        x1_std = sem("x1_std")
        m_steps = sem("m_steps")
        m_ready = sem("m_ready")
        m_kept = sem("m_kept")
        m_turned = sem("m_turned")
        mT_ready = sem("mT_ready")
        logit_ready = sem("logit_ready")
        pick_steps = sem("pick_steps")
        gap_ready = sem("gap_ready")
        exp_ready = sem("exp_ready")
        sent_ready = sem("sent_ready")
        both_ready = sem("both_ready")
        run_ready = sem("run_ready")
        place_ready = sem("place_ready")
        place_steps = sem("place_steps")
        slot_ready = sem("slot_ready")
        begun = sem("scatters_begun")
        scattered = [sem(f"scattered{k}") for k in range(2)]
        counted = sem("counted")
        tail_ready = sem("tail_ready")
        tails_out = sem("tails_out")
        list_steps = sem("list_steps")

        block = ctx.enter_context(nc.Block())
        CONST_LOADS = 6

        def clear_tails(engine, first):
            engine.wait_ge(tail_ready, 1)
            for e in range(first, E, 2):
                start = engine.value_load(tail[0:1, e:e + 1], min_val=0, max_val=E * QUEUE - TR)
                engine.dma_start(rows_in[bass.ds(start, TR), :].rearrange("(p u) c -> p (u c)", p=P),
                                 zeros[:]).then_inc(tails_out, 16)

        @block.sync
        def _(sp):
            for dst, src in (
                (W_sb[:], W.rearrange("(k p) o -> p k o", p=P)),
                (rows[:, 0:C], b.rearrange("(a c) -> a c", a=1)),
                (rows[:, C:C + E], gate_b.rearrange("(a c) -> a c", a=1)),
                (gw_sb[:], gate_w),
                (grid[:], moe_small),
                (earlier[:], gate_consts),
            ):
                sp.dma_start(dst, src).then_inc(consts_in, 16)
            sp.wait_ge(pool_ready, 2)
            spare = rows_in[E * QUEUE:, :].rearrange("(p r) c -> p (r c)", p=P)
            sp.dma_start(spare, zeros[:]).then_inc(spare_out, 16)
            for dst, src in expert_loads:
                sp.dma_start(dst, src).then_inc(weights_in, 16)
            sp.wait_ge(spare_out, 16)
            sp.wait_ge(weights_in, 16 * len(expert_loads))
            clear_tails(sp, 0)
            sp.wait_ge(tails_out, 16 * E)

        LAGS = 6

        def stages(engine, step):
            for j in range(LAGS):
                step(0, j)
            with engine.Fori(LAGS // 2, GROUPS // 2) as it:
                step(it, 0)
                step(it, 1)
            for j in range(LAGS):
                step(GROUPS // 2, j)

        def exists(it, k, lag):
            if not isinstance(it, int):
                return True
            return 0 <= 2 * it + k - lag < GROUPS

        def place_of(it, k, lag):
            return it * 2 + (k - lag), (k - lag) % 2, it + (k - lag) // 2

        @block.gpsimd
        def _(pool):
            g = nc.gpsimd
            g.memset(ones[:], 1.0).then_inc(pool_ready, 1)
            g.memset(zeros[:], 0.0).then_inc(pool_ready, 1)

            def step(it, k):
                if not exists(it, k, 6):
                    return
                i, h, _ = place_of(it, k, 6)
                pool.wait_ge(sent_ready, i + 1)
                pool.wait_ge(slot_ready, i + 1)
                pool.sem_inc(begun, 1)
                for c in range(2):
                    for a in range(GT):
                        col = slice(c * GT + a, c * GT + a + 1)
                        pool.indirect_dma_start(
                            out=rows_in, in_=send[:, h, a, :], in_offset=None,
                            out_offset=bass.IndirectOffsetOnAxis(ap=slot[:, h, col], axis=0),
                        ).then_inc(scattered[h], 16)
            stages(pool, step)
            for h in range(2):
                pool.wait_ge(scattered[h], 16 * 2 * GT * (GROUPS // 2))

        @block.vector
        def _(dve):
            v = nc.vector

            def stage_n(it, k):
                i, h, _ = place_of(it, k, 0)
                if not (isinstance(i, int) and i < 2):
                    dve.wait_ge(nT_turned, i - 1)
                for a in range(GT):
                    col = bass.ds(i * GT + a, 1)
                    ins = v.tensor_scalar(n_grp[:, h, a, :], x_sb[:, col, :], mean_sb[:, col, 0], rstd[:, col],
                                          ALU.subtract, ALU.mult)
                ins.then_inc(n_taken, 1)

            def stage_x1(it, k):
                i, h, _ = place_of(it, k, 2)
                tiles = bass.ds(i * GT, GT)
                dve.sem_clear(x1_steps)
                dve.wait_ge(lin_ready, i + 1)
                v.scalar_tensor_tensor(x_sb[:, tiles, :], lin[h][:], 0.0, x_sb[:, tiles, :], ALU.max,
                                       ALU.add).then_inc(x1_steps, 1)
                dve.wait_ge(x1_steps, 1)
                for a in range(GT):
                    ins = v.bn_stats(st[:, a, :], x_sb[:, bass.ds(i * GT + a, 1), :])
                ins.then_inc(x1_steps, 1)
                dve.wait_ge(x1_steps, 2)
                for a in range(GT):
                    ins = v.bn_aggr(mv[:, h, a, :], st[:, a, :])
                ins.then_inc(x1_stats, 1)

            def stage_m(it, k):
                i, h, half = place_of(it, k, 2)
                dve.sem_clear(m_steps)
                dve.wait_ge(x1_std, i + 1)
                v.reciprocal(rs[:], sd[:, h, :]).then_inc(m_steps, 1)
                if not (isinstance(i, int) and i < 2):
                    dve.wait_ge(m_turned, i - 1)
                    dve.wait_ge(m_kept, i - 1)
                dve.wait_ge(m_steps, 1)
                for a in range(GT):
                    ins = v.tensor_scalar(m[:, h, a, :], x_sb[:, bass.ds(i * GT + a, 1), :], mv[:, h, a, 0:1],
                                          rs[:, a:a + 1], ALU.subtract, ALU.mult)
                ins.then_inc(m_ready, 1)

            def stage_top(it, k):
                i, h, _ = place_of(it, k, 4)
                dve.sem_clear(pick_steps)
                dve.wait_ge(logit_ready, i + 1)
                v.tensor_copy(logit[:], logit_ps[h][:]).then_inc(pick_steps, 1)
                dve.wait_ge(pick_steps, 1)
                for a in range(GT):
                    ins = v.max(top2[:, h, a, :], logit[:, a, :])
                ins.then_inc(pick_steps, 1)
                dve.wait_ge(pick_steps, 2)
                v.tensor_tensor(gap[:, bass.ds(i * GT, GT)], top2[:, h, :, 1], top2[:, h, :, 0],
                                ALU.subtract).then_inc(gap_ready, 1)
                for a in range(GT):
                    ins = v.max_index(pick[:, a, :], top2[:, h, a, :], logit[:, a, :])
                ins.then_inc(pick_steps, 1)
                dve.wait_ge(pick_steps, 3)
                v.tensor_copy(pickf[:], pick[:, :, 0:2].rearrange("p a c -> p c a")).then_inc(pick_steps, 1)

            def stage_pick(it, k):
                i, h, _ = place_of(it, k, 4)
                dve.wait_ge(pick_steps, 4)
                for c in range(2):
                    v.tensor_tensor(chosen[:, bass.ds(i * (2 * GT) + c * GT, GT), :],
                                    expert_ids.unsqueeze(1).to_broadcast([P, GT, E]),
                                    pickf[:, c, :].unsqueeze(2).to_broadcast([P, GT, E]),
                                    ALU.is_equal).then_inc(pick_steps, 1)
                if not (isinstance(i, int) and i < 2):
                    dve.wait_ge(place_ready, i - 1)
                dve.wait_ge(pick_steps, 6)
                v.tensor_tensor(both[:, h, :, :], chosen[:, bass.ds(i * (2 * GT), GT), :],
                                chosen[:, bass.ds(i * (2 * GT) + GT, GT), :], ALU.add).then_inc(both_ready, 1)
                dve.wait_ge(both_ready, i + 1)
                dve.wait_ge(run_ready, i + 1)
                with nc.allow_low_precision(reason="counts up to 128 are exact"):
                    v.tensor_reduce(group_sum[:], both[:, h, :, :].rearrange("p a e -> p e a"), AX.X,
                                    ALU.add).then_inc(pick_steps, 1)
                dve.wait_ge(pick_steps, 7)
                v.tensor_tensor(run[:, bass.ds(i + 1, 1), :], run[:, bass.ds(i, 1), :],
                                group_sum[:].unsqueeze(1), ALU.add).then_inc(run_ready, 1)

            def stage_place(it, k):
                i, h, half = place_of(it, k, 6)
                these = bass.ds(i * (2 * GT), 2 * GT)
                dve.sem_clear(place_steps)
                if not (isinstance(i, int) and i < 2):
                    dve.wait_ge(scattered[h], half * (16 * 2 * GT))
                dve.wait_ge(place_ready, i + 1)
                v.tensor_tensor(place[:], place_ps[h][:], queue_start, ALU.add).then_inc(place_steps, 1)
                dve.wait_ge(place_steps, 1)
                v.tensor_tensor(picked[:].rearrange("p c a e -> p c (a e)"),
                                chosen[:, these, :].rearrange("p (c a) e -> p c (a e)", c=2),
                                place[:].rearrange("p a e -> p (a e)").unsqueeze(1).to_broadcast([P, 2, GT * E]),
                                ALU.mult).then_inc(place_steps, 1)
                dve.wait_ge(place_steps, 2)
                v.tensor_reduce(place_all[:, these], picked[:].rearrange("p c a e -> p (c a) e"), AX.X,
                                ALU.add).then_inc(place_steps, 1)
                dve.wait_ge(place_steps, 3)
                v.tensor_copy(slot[:, h, :], place_all[:, these]).then_inc(slot_ready, 1)

            def step(it, k):
                if exists(it, k, 2):
                    stage_x1(it, k)
                if exists(it, k, 6):
                    stage_place(it, k)
                if exists(it, k, 4):
                    stage_top(it, k)
                if exists(it, k, 0):
                    stage_n(it, k)
                if exists(it, k, 4):
                    stage_pick(it, k)
                if exists(it, k, 2):
                    stage_m(it, k)

            v.memset(run[:, 0, :], 0.0).then_inc(run_ready, 1)
            v.memset(row["ones"][:], 1.0).then_inc(list_steps, 1)
            dve.wait_ge(consts_in, 16 * CONST_LOADS)
            stages(dve, step)

            dve.wait_ge(counted, 1)
            v.tensor_copy(count[:], place_ps[0][:, 0, :]).then_inc(list_steps, 1)
            n = 1

            def after(instruction):
                nonlocal n
                n += 1
                instruction.then_inc(list_steps, 1)
                dve.wait_ge(list_steps, n)
            dve.wait_ge(list_steps, 2)
            n = 2
            v.tensor_tensor(tail[:], count[0:1, :], queue_start[0:1, 0, :], ALU.add).then_inc(tail_ready, 1)

            after(v.tensor_scalar(row_int[:], count[:], float(TR - 1), None, ALU.add))
            after(v.tensor_scalar(row_int[:], row_int[:], TR.bit_length() - 1, None, ALU.arith_shift_right))
            after(v.tensor_copy(row["tiles"][:], row_int[:]))
            after(v.tensor_tensor_scan(row["upto"][:], row["ones"][:], row["tiles"][:], 0.0, ALU.mult, ALU.add))
            wide = [1, MOE_TILES, E]
            after(v.tensor_tensor(past[:], number.unsqueeze(2).to_broadcast(wide),
                                  row["upto"][0:1, :].unsqueeze(1).to_broadcast(wide), ALU.is_ge))
            after(v.tensor_reduce(line["expert"][:], past[:], AX.X, ALU.add))
            after(v.tensor_tensor(past[:], past[:], row["tiles"][0:1, :].unsqueeze(1).to_broadcast(wide), ALU.mult))
            after(v.tensor_reduce(line["before"][:], past[:], AX.X, ALU.add))
            after(v.tensor_tensor(line["index"][:], number, line["before"][:], ALU.subtract))
            after(v.tensor_scalar(line["row"][:], line["expert"][:], float(QUEUE // TR), None, ALU.mult))
            after(v.tensor_tensor(line["row"][:], line["row"][:], line["index"][:], ALU.add))
            after(v.tensor_scalar(tile_row[:], line["row"][:], float(ROW_TILES - 1), None, ALU.min))
            after(v.tensor_scalar(tile_expert[:], line["expert"][:], float(E - 1), None, ALU.min))
            after(v.tensor_tensor(row["moved"][:], row["upto"][:], row["tiles"][:], ALU.subtract))
            after(v.scalar_tensor_tensor(row["moved"][:], row["moved"][:], float(TR), queue_start[:, 0, :],
                                         ALU.mult, ALU.subtract))
            after(v.tensor_tensor(moved[:], chosen[:], row["moved"][:].unsqueeze(1).to_broadcast([P, 2 * TILES, E]),
                                  ALU.mult))
            after(v.tensor_reduce(move[:], moved[:], AX.X, ALU.add))
            after(v.tensor_tensor(slot_all[:], move[:], place_all[:], ALU.add))
            dve.wait_ge(exp_ready, 1)
            after(v.tensor_scalar(den[:], eg[:], 1.0, None, ALU.add))
            after(v.reciprocal(weight_all[:, 0, :], den[:]))
            after(v.tensor_tensor(weight_all[:, 1, :], eg[:], weight_all[:, 0, :], ALU.mult))

        @block.scalar
        def _(act):
            s = nc.scalar

            def step(it, k):
                if exists(it, k, 1):
                    i, h, _ = place_of(it, k, 1)
                    if not (isinstance(i, int) and i < 2):
                        act.wait_ge(lin_ready, i - 1)
                    s.activation(aggT[:, h, :, :], agg_T[:, bass.ds(i * GN, GN)].rearrange("p (a q) -> p a q", a=GT),
                                 ACT.Copy, scale=1.0 / SCALE).then_inc(aggT_ready, 1)
                    act.wait_ge(nT_turned, i + 1)
                    s.copy(nT[:, h, :, :], turned[:]).then_inc(nT_ready, 1)
                if exists(it, k, 3):
                    i, h, _ = place_of(it, k, 3)
                    if not (isinstance(i, int) and i < 2):
                        act.wait_ge(logit_ready, i - 1)
                    act.wait_ge(m_turned, i + 1)
                    s.copy(mT[:, h, :, :], m_turned_ps[:]).then_inc(mT_ready, 1)
                if exists(it, k, 2):
                    i, h, _ = place_of(it, k, 2)
                    act.wait_ge(x1_stats, i + 1)
                    s.activation(sd[:, h, :], mv[:, h, :, 1], ACT.Sqrt, bias=eps[:]).then_inc(x1_std, 1)
                if exists(it, k, 3):
                    i, h, _ = place_of(it, k, 3)
                    act.wait_ge(m_ready, i + 1)
                    s.copy(m_all[:, bass.ds(i * GT, GT), :], m[:, h, :, :]).then_inc(m_kept, 1)
                if exists(it, k, 5):
                    i, h, half = place_of(it, k, 5)
                    act.wait_ge(m_kept, i + 1)
                    if not (isinstance(i, int) and i < 2):
                        act.wait_ge(scattered[h], half * (16 * 2 * GT))
                    s.copy(send[:, h, :, :], m_all[:, bass.ds(i * GT, GT), :]).then_inc(sent_ready, 1)
            stages(act, step)
            act.wait_ge(gap_ready, GROUPS)
            s.activation(eg[:], gap[:], ACT.Exp).then_inc(exp_ready, 1)
            clear_tails(act, 1)

        @block.tensor
        def _(pe):
            t = nc.tensor

            def step(it, k):
                if exists(it, k, 1):
                    i, h, _ = place_of(it, k, 1)
                    if not (isinstance(i, int) and i < 1):
                        pe.wait_ge(nT_ready, i)
                    pe.wait_ge(n_taken, i + 1)
                    for a in range(GT):
                        ins = t.transpose(turned[:, a, :], n_grp[:, h, a, :], ident)
                    ins.then_inc(nT_turned, 1)
                if exists(it, k, 3):
                    i, h, _ = place_of(it, k, 3)
                    if not (isinstance(i, int) and i < 1):
                        pe.wait_ge(mT_ready, i)
                    pe.wait_ge(m_ready, i + 1)
                    for a in range(GT):
                        ins = t.transpose(m_turned_ps[:, a, :], m[:, h, a, :], ident)
                    ins.then_inc(m_turned, 1)
                if exists(it, k, 1):
                    i, h, _ = place_of(it, k, 1)
                    if not (isinstance(i, int) and i < 2):
                        pe.wait_ge(x1_stats, i - 1)
                    pe.wait_ge(aggT_ready, i + 1)
                    pe.wait_ge(nT_ready, i + 1)
                    for a in range(GT):
                        t.matmul(lin[h][:, a, :], nT[:, h, a, :], W_sb[:, 0, :], start=True, stop=False)
                        t.matmul(lin[h][:, a, :], aggT[:, h, a, :], W_sb[:, 1, :], start=False, stop=False)
                        ins = t.matmul(lin[h][:, a, :], ones[:], rows[:, 0:C], start=False, stop=True)
                    ins.then_inc(lin_ready, 1)
                if exists(it, k, 5):
                    i, h, _ = place_of(it, k, 5)
                    if not (isinstance(i, int) and i < 2):
                        pe.wait_ge(slot_ready, i - 1)
                    pe.wait_ge(both_ready, i + 1)
                    pe.wait_ge(run_ready, i + 1)
                    for a in range(GT):
                        dst = place_ps[h][:, a, :]
                        t.matmul(dst, EARLIER, both[:, h, a, :], start=True, stop=False)
                        for c in range(a):
                            t.matmul(dst, ALL, both[:, h, c, :], start=False, stop=False)
                        ins = t.matmul(dst, ALL, run[:, bass.ds(i, 1), :].rearrange("p a e -> p (a e)"),
                                       start=False, stop=True)
                    ins.then_inc(place_ready, 1)
                if exists(it, k, 3):
                    i, h, _ = place_of(it, k, 3)
                    if not (isinstance(i, int) and i < 2):
                        pe.wait_ge(gap_ready, i - 1)
                    pe.wait_ge(mT_ready, i + 1)
                    for a in range(GT):
                        t.matmul(logit_ps[h][:, a, :], mT[:, h, a, :], gw_sb[:], start=True, stop=False)
                        ins = t.matmul(logit_ps[h][:, a, :], ones[:], rows[:, C:C + E],
                                       start=False, stop=True)
                    ins.then_inc(logit_ready, 1)
            pe.wait_ge(consts_in, 16 * CONST_LOADS)
            pe.wait_ge(pool_ready, 2)
            stages(pe, step)
            pe.wait_ge(run_ready, GROUPS + 1)
            pe.wait_ge(slot_ready, GROUPS)
            t.matmul(place_ps[0][:, 0, :], ALL, run[:, GROUPS, :], start=True, stop=True).then_inc(counted, 1)


def experts(nc, w1_sb, b1_sb, w2_sb, b2_sb, const, tile_row, tile_expert, rows_in, rows_out):
    with ExitStack() as ctx:
        def sb(name, shape, dt=F32):
            return ctx.enter_context(nc.sbuf_tensor(name, shape, dt))

        def ps(name, shape):
            return ctx.enter_context(nc.psum_tensor(name, shape, F32))

        def sem(name):
            return ctx.enter_context(nc.semaphore(name))

        ident = const[:, 0:P]
        x_in = sb("x_in", [P, SLOTS, HALVES, C])
        xT = sb("xT", [P, 2, HALVES, P])
        h_in = sb("h_in", [P, 2, HALVES, F])
        hT = sb("hT", [P, 2, HALVES, FC, P])
        o_sb = sb("o_sb", [P, SLOTS, HALVES, C])
        xT_ps = [ps(f"xT_ps{k}", [P, HALVES, P]) for k in range(2)]
        h_ps = [ps(f"h_ps{k}", [P, HALVES, F]) for k in range(2)]
        hT_ps = [ps(f"hT_ps{k}", [P, HALVES, FC, P]) for k in range(2)]
        o_ps = [ps(f"o_ps{k}", [P, HALVES, C]) for k in range(2)]

        loaded = [sem(f"loaded{k}") for k in range(SLOTS)]
        stored = [sem(f"stored{k}") for k in range(SLOTS)]
        x_turned = sem("x_turned")
        xT_ready = sem("xT_ready")
        inner_ready = sem("inner_ready")
        biased = sem("biased")
        h_turned = sem("h_turned")
        relu_ready = sem("relu_ready")
        outer_ready = sem("outer_ready")
        o_ready = sem("o_ready")

        tiles_in = rows_in.rearrange("(t p u) c -> t p u c", p=P, u=HALVES)
        tiles_out = rows_out.rearrange("(t p u) c -> t p u c", p=P, u=HALVES)
        block = ctx.enter_context(nc.Block())
        LAST = 3

        def stages(engine, step):
            for k in range(SLOTS):
                step(0, k)
            with engine.Fori(1, MOE_TILES // SLOTS) as it:
                for k in range(SLOTS):
                    step(it, k)
            for k in range(LAST):
                step(MOE_TILES // SLOTS, k)

        def tile_of(it, k, lag):
            if isinstance(it, int) and not 0 <= SLOTS * it + k - lag < MOE_TILES:
                return None
            return it * SLOTS + (k - lag)

        def at(tile):
            return slice(tile, tile + 1) if isinstance(tile, int) else bass.ds(tile, 1)

        def expert_of(engine, tile):
            return engine.value_load(tile_expert[0:1, at(tile)], min_val=0, max_val=E - 1)

        def row_of(engine, tile):
            return engine.value_load(tile_row[0:1, at(tile)], min_val=0, max_val=ROW_TILES - 1)

        @block.sync
        def _(sp):
            for k in range(SLOTS):
                sp.sem_inc(stored[k], 16)

            def load(it, k, lag):
                tile = tile_of(it, k, lag)
                if tile is None:
                    return
                slot = (k - lag) % SLOTS
                row = row_of(sp, tile)
                if not (isinstance(tile, int) and tile < SLOTS):
                    sp.wait_ge(x_turned, tile - SLOTS + 1)
                sp.dma_start(x_in[:, slot, :, :], tiles_in[row]).then_inc(loaded[slot], 16)

            def store(it, k):
                tile = tile_of(it, k, LAST)
                if tile is None:
                    return
                slot = (k - LAST) % SLOTS
                sp.wait_ge(o_ready, tile + 1)
                sp.dma_start(tiles_out[tile], o_sb[:, slot, :, :]).then_inc(stored[slot], 16)

            for k in range(AHEAD):
                load(0, k, 0)

            def step(it, k):
                load(it, k, -AHEAD)
                store(it, k)
            for k in range(SLOTS):
                step(0, k)
            with sp.Fori(1, MOE_TILES // SLOTS - 1) as it:
                for k in range(SLOTS):
                    step(it, k)
            for k in range(SLOTS + LAST):
                step(MOE_TILES // SLOTS - 1, k)
            for k in range(SLOTS):
                sp.wait_ge(stored[k], 16 * (MOE_TILES // SLOTS + 1))

        @block.tensor
        def _(pe):
            t = nc.tensor

            def step(it, k):
                if (tile := tile_of(it, k, 0)) is not None:
                    pe.wait_ge(loaded[k], it * 16 + 16)
                    for u in range(HALVES):
                        ins = t.transpose(xT_ps[k % 2][:, u, :], x_in[:, k, u, :], ident)
                    ins.then_inc(x_turned, 1)
                if (tile := tile_of(it, k, 1)) is not None:
                    par = (k - 1) % 2
                    e = expert_of(pe, tile)
                    pe.wait_ge(xT_ready, tile + 1)
                    w = w1_sb[:, bass.ds(e, 1), :].rearrange("p a f -> p (a f)")
                    for u in range(HALVES):
                        ins = t.matmul(h_ps[par][:, u, :], xT[:, par, u, :], w, start=True, stop=True)
                    ins.then_inc(inner_ready, 1)
                if (tile := tile_of(it, k, 2)) is not None:
                    par = (k - 2) % 2
                    pe.wait_ge(biased, tile + 1)
                    for u in range(HALVES):
                        for f in range(FC):
                            ins = t.transpose(hT_ps[par][:, u, f, :], h_in[:, par, u, f * P:(f + 1) * P], ident)
                    ins.then_inc(h_turned, 1)
                if (tile := tile_of(it, k, 3)) is not None:
                    par = (k - 3) % 2
                    e = expert_of(pe, tile)
                    if not (isinstance(tile, int) and tile < 2):
                        pe.wait_ge(o_ready, tile - 1)
                    pe.wait_ge(relu_ready, tile + 1)
                    for u in range(HALVES):
                        for f in range(FC):
                            w = w2_sb[:, bass.ds(e, 1), f * C:(f + 1) * C].rearrange("p a c -> p (a c)")
                            ins = t.matmul(o_ps[par][:, u, :], hT[:, par, u, f, :], w,
                                           start=(f == 0), stop=(f == FC - 1))
                    ins.then_inc(outer_ready, 1)
            stages(pe, step)

        @block.scalar
        def _(act):
            s = nc.scalar

            def step(it, k):
                if (tile := tile_of(it, k, 0)) is not None:
                    act.wait_ge(x_turned, tile + 1)
                    s.copy(xT[:, k % 2, :, :], xT_ps[k % 2][:]).then_inc(xT_ready, 1)
                if (tile := tile_of(it, k, 2)) is not None:
                    par = (k - 2) % 2
                    act.wait_ge(h_turned, tile + 1)
                    s.activation(hT[:, par, :, :, :], hT_ps[par][:], ACT.Relu).then_inc(relu_ready, 1)
            stages(act, step)

        @block.vector
        def _(dve):
            v = nc.vector

            def step(it, k):
                if (tile := tile_of(it, k, 1)) is not None:
                    par = (k - 1) % 2
                    e = expert_of(dve, tile)
                    dve.wait_ge(inner_ready, tile + 1)
                    v.tensor_tensor(h_in[:, par, :, :], h_ps[par][:],
                                    b1_sb[:, bass.ds(e, 1), :].to_broadcast([P, HALVES, F]),
                                    ALU.add).then_inc(biased, 1)
                if (tile := tile_of(it, k, 3)) is not None:
                    par, slot = (k - 3) % 2, (k - 3) % SLOTS
                    e = expert_of(dve, tile)
                    dve.wait_ge(stored[slot], (it + (k - 3) // SLOTS) * 16 + 16)
                    dve.wait_ge(outer_ready, tile + 1)
                    v.tensor_tensor(o_sb[:, slot, :, :], o_ps[par][:],
                                    b2_sb[:, bass.ds(e, 1), :].to_broadcast([P, HALVES, C]),
                                    ALU.add).then_inc(o_ready, 1)
            stages(dve, step)


def results(nc, gamma, beta, out, x_sb, m_all, weight_all, slot_all, rows_out, eps):
    with ExitStack() as ctx:
        def sb(name, shape, dt=F32):
            return ctx.enter_context(nc.sbuf_tensor(name, shape, dt))

        def sem(name):
            return ctx.enter_context(nc.semaphore(name))

        gamma_sb = sb("gamma_sb", [P, C])
        beta_sb = sb("beta_sb", [P, C])
        names = sb("names", [P, GB2, 2 * GT], I32)
        got = sb("got2", [P, GB2, 2, GT, C])
        y = sb("y", [P, 2, GT, C])
        st = sb("st2", [P, GT, 6])
        mv = sb("mv2", [P, 2, GT, 2])
        sd = sb("sd2", [P, 2, GT])
        rs = sb("rs2", [P, GT])
        z = sb("z", [P, GT, C])
        xb = sb("xb", [P, GT, C])
        res = sb("res", [P, 2, GT, C])

        consts_in = sem("res_consts_in")
        names_ready = sem("names_ready")
        names_seen = sem("names_seen")
        got_free = sem("got_free")
        fetched = [sem(f"fetched{k}") for k in range(GB2)]
        y_steps = sem("y_steps")
        y_stats = sem("y_stats")
        y_std = sem("y_std")
        res_steps = sem("res_steps")
        res_ready = sem("res_ready")
        out_stored = [sem(f"out_stored{k}") for k in range(2)]
        out_g = out.rearrange("b (g a p) c -> (b g) p a c", p=P, a=GT)
        block = ctx.enter_context(nc.Block())

        def pairs(engine, step):
            step(0, 0)
            step(0, 1)
            with engine.Fori(1, GROUPS // 2) as it:
                step(it, 0)
                step(it, 1)
            step(GROUPS // 2, 0)

        def exists(it, k, lag):
            return not isinstance(it, int) or 0 <= 2 * it + k - lag < GROUPS

        @block.sync
        def _(sp):
            sp.dma_start(gamma_sb[:], gamma.partition_broadcast(P)).then_inc(consts_in, 16)
            sp.dma_start(beta_sb[:], beta.partition_broadcast(P)).then_inc(consts_in, 16)
            for h in range(2):
                sp.sem_inc(out_stored[h], 16)
            with sp.Fori(0, GROUPS // 2) as it:
                for h in range(2):
                    sp.wait_ge(res_ready, it * 2 + (h + 1))
                    sp.dma_start(out_g[it * 2 + h], res[:, h, :, :]).then_inc(out_stored[h], 16)
            for h in range(2):
                sp.wait_ge(out_stored[h], 16 * (GROUPS // 2 + 1))

        @block.gpsimd
        def _(pool):
            g = nc.gpsimd
            pool.sem_inc(got_free, GB2)
            with pool.Fori(0, GROUPS // GB2) as it:
                for k in range(GB2):
                    i = it * GB2 + k
                    pool.wait_ge(got_free, i + 1)
                    g.tensor_copy(names[:, k, :], slot_all[:, bass.ds(i * (2 * GT), 2 * GT)]).then_inc(names_ready, 1)
                    pool.wait_ge(names_ready, i + 1)
                    pool.sem_inc(names_seen, 1)
                    for c in range(2):
                        for a in range(GT):
                            col = slice(c * GT + a, c * GT + a + 1)
                            pool.indirect_dma_start(
                                out=got[:, k, c, a, :], out_offset=None, in_=rows_out,
                                in_offset=bass.IndirectOffsetOnAxis(ap=names[:, k, col], axis=0),
                            ).then_inc(fetched[k], 16)

        @block.scalar
        def _(act):
            s = nc.scalar
            with act.Fori(0, GROUPS // 2) as it:
                for h in range(2):
                    act.wait_ge(y_stats, it * 2 + (h + 1))
                    s.activation(sd[:, h, :], mv[:, h, :, 1], ACT.Sqrt, bias=eps[:]).then_inc(y_std, 1)

        @block.vector
        def _(dve):
            v = nc.vector

            def stage_y(it, h):
                i = it * 2 + h
                dve.sem_clear(y_steps)
                dve.wait_ge(fetched[h], it * (16 * 2 * GT) + 16 * 2 * GT)
                for c in range(2):
                    for a in range(GT):
                        col = bass.ds(i * GT + a, 1)
                        before = m_all[:, col, :].rearrange("p a c -> p (a c)") if c == 0 else y[:, h, a, :]
                        ins = v.scalar_tensor_tensor(y[:, h, a, :], got[:, h, c, a, :], weight_all[:, c, col],
                                                     before, ALU.mult, ALU.add)
                    ins.then_inc(y_steps, 1)
                    dve.wait_ge(y_steps, c + 1)
                dve.sem_inc(got_free, 1)
                for a in range(GT):
                    ins = v.bn_stats(st[:, a, :], y[:, h, a, :])
                ins.then_inc(y_steps, 1)
                dve.wait_ge(y_steps, 3)
                for a in range(GT):
                    ins = v.bn_aggr(mv[:, h, a, :], st[:, a, :])
                ins.then_inc(y_stats, 1)

            def stage_result(it, k):
                h = (k - 1) % 2
                i = it * 2 + (k - 1)
                dve.sem_clear(res_steps)
                dve.wait_ge(res_ready, i)
                wide = [P, GT, C]
                v.tensor_tensor(xb[:], x_sb[:, bass.ds(i * GT, GT), :],
                                beta_sb[:].unsqueeze(1).to_broadcast(wide), ALU.add).then_inc(res_steps, 1)
                dve.wait_ge(y_std, i + 1)
                v.reciprocal(rs[:], sd[:, h, :]).then_inc(res_steps, 1)
                dve.wait_ge(res_steps, 2)
                for a in range(GT):
                    ins = v.tensor_scalar(z[:, a, :], y[:, h, a, :], mv[:, h, a, 0:1], rs[:, a:a + 1],
                                          ALU.subtract, ALU.mult)
                ins.then_inc(res_steps, 1)
                dve.wait_ge(res_steps, 3)
                v.tensor_tensor(z[:], z[:], gamma_sb[:].unsqueeze(1).to_broadcast(wide),
                                ALU.mult).then_inc(res_steps, 1)
                dve.wait_ge(res_steps, 4)
                dve.wait_ge(out_stored[h], (it + (k - 1) // 2) * 16 + 16)
                v.tensor_tensor(res[:, h, :, :], z[:], xb[:], ALU.add).then_inc(res_ready, 1)

            def step(it, k):
                if exists(it, k, 0):
                    stage_y(it, k)
                if exists(it, k, 1):
                    stage_result(it, k)
            dve.wait_ge(consts_in, 32)
            pairs(dve, step)


INPUTS = ("x", "adj", "L0_gnn_W", "L0_gnn_b", "L0_ffn_gate_w", "L0_ffn_gate_b", "L0_ffn_w1", "L0_ffn_b1",
          "L0_ffn_w2", "L0_ffn_b2", "L0_ffn_gamma", "L0_ffn_beta")


def kernel(**inputs):
    import concourse.bacc as bacc
    from concourse.bass_utils import run_bass_kernel_spmd

    laid = {name: np.ascontiguousarray(inputs[name]) for name in INPUTS}
    adj_t = np.ascontiguousarray(laid["adj"].reshape(B, GB, GN, N).transpose(0, 1, 3, 2).reshape(GROUPS, N, GN))
    laid = {"x": laid.pop("x"), "adj": laid.pop("adj"), "adj_t": adj_t, **laid}
    laid.update(shape_constants())
    laid.update(moe_constants())

    nc = bacc.Bacc("TRN2", target_bir_lowering=False, num_devices=1)
    args = [nc.dram_tensor(f"in_{k}", v.shape, mybir.dt.from_np(v.dtype), kind="ExternalInput").ap()
            for k, v in laid.items()]
    out = nc.dram_tensor("out", (B, N, C), F32, kind="ExternalOutput").ap()
    build(nc, *args, out)
    r = run_bass_kernel_spmd(nc, [{f"in_{k}": v for k, v in laid.items()}], core_ids=[0])
    return r.results[0]["out"]
```

```python
from contextlib import ExitStack

import numpy as np

import concourse.bass as bass
from concourse import mybir

F32 = mybir.dt.float32
F16 = mybir.dt.float16
I32 = mybir.dt.int32
U32 = mybir.dt.uint32
ALU = mybir.AluOpType
ACT = mybir.ActivationFunctionType
AX = mybir.AxisListType

P = 128
B, N, C = 8, 1024, 128
S = 25
E, F = 16, 256
FC = F // P
TILES = B * N // P
GT = 4
GROUPS = TILES // GT
GN = GT * P
BT = N // P
GB = BT // GT
ROWS = N + 1
EPS = 1e-5
LOWEST = -3.0e38
TOP = 8
ROUNDS = -(-(S + 1) // TOP)

RUNS = N // P
R, L = 5, 5
HIT = 64.0
DROP = 64.0
SCALE = 1024.0
PERIODS = R
PU = RUNS // 2 + 1
MIDDLE = PU // 2
UNITS = PERIODS * PU
MASKS = 2 * PERIODS
RING = 3
BANKS = [u % RING for u in range(UNITS - 1)] + [(UNITS - 1) % RING if (UNITS - 1) % RING else 1]
MASK_RING = 5
assert R == L and MASKS % MASK_RING == 0 and RUNS % 2 == 0 and S < HIT


def shape_constants():
    first = np.zeros((P, 2 * P), np.float32)
    first[:, :P] = np.eye(P)
    first[:, P:P + E] = np.arange(E)
    first[:, P + E:P + E + TILES] = (np.arange(TILES) // BT) * ROWS + N
    priority = np.broadcast_to((N - np.arange(N)).astype(np.float16), (P, N))
    count = np.triu(np.ones((P, P)))
    counting = np.stack([count, count + HIT * np.eye(P), np.ones((P, P)), -DROP * np.eye(P)], 1)
    return {"small": first, "priority": np.ascontiguousarray(priority),
            "counting": counting.astype(np.float16)}


HALVES = 2
TR = HALVES * P
QUEUE = B * N + TR
MOE_TILES = 2 * B * N // TR + E
ROW_TILES = E * QUEUE // TR + 1
SLOTS = 4
AHEAD = 3
FETCHES = 4
GRID_COLS = GT * E + 2 * TILES + MOE_TILES
CW = C + 1
NOWHERE = 2 * B * N
NOBODY = float(1 << 20)
assert NOWHERE + MOE_TILES * TR < NOBODY
assert QUEUE % TR == 0 and MOE_TILES % SLOTS == 0 and TR == 1 << (TR.bit_length() - 1)


def moe_constants():
    start = np.arange(E) * QUEUE
    grid = np.zeros((P, GRID_COLS), np.float32)
    grid[:, 0:GT * E] = np.tile(start, GT)
    token = (np.arange(TILES) * P).reshape(GROUPS, 1, GT) + np.arange(2).reshape(1, 2, 1) * B * N
    grid[:, GT * E:GT * E + 2 * TILES] = token.reshape(-1) + np.arange(P)[:, None]
    grid[:, GT * E + 2 * TILES:] = np.arange(MOE_TILES)
    before = np.stack([np.triu(np.ones((P, P)), 1), np.ones((P, P))], 1)
    nowhere = NOWHERE + np.arange(MOE_TILES * TR).reshape(MOE_TILES, P, HALVES).transpose(1, 0, 2)
    return {"moe_small": grid, "gate_consts": before.astype(np.float16),
            "nowhere_rows": np.ascontiguousarray(nowhere.astype(np.float32))}


def ranking_items():
    order = [("all", 0)]
    for b in range(1, RUNS):
        order += [("all", b), ("run", b - 1)]
    order += [("run", RUNS - 1), ("degree", 0)]
    order += [("rest", b) for b in range(RUNS)] + [("rest_count", 0)]
    bank = {"all": lambda b: 0, "run": lambda b: 1, "degree": lambda b: 0,
            "rest": lambda b: (b + 1) % 2, "rest_count": lambda b: 1}
    return [(kind, b, bank[kind](b)) for kind, b in order]


ITEMS = ranking_items()
AT = {(kind, b): n for n, (kind, b, _) in enumerate(ITEMS)}
BEHIND = {}
EDGES_AT = (RUNS + 6, RUNS + 9)
for _kind, _b, _ in ITEMS:
    BEHIND[_kind, _b] = {"all": _b, "run": _b + 1, "degree": RUNS + 1, "rest": RUNS + 4 + _b,
                         "rest_count": 2 * RUNS + 4}[_kind]
assert max(BEHIND.values()) <= UNITS - PU


def build(nc, x, adj, adj_t, W, b, gate_w, gate_b, w1, b1, w2, b2, gamma, beta, small, priority, counting,
          moe_small, gate_consts, nowhere_rows, out):
    with ExitStack() as ctx:
        def sb(name, shape, dt=F32):
            return ctx.enter_context(nc.sbuf_tensor(name, shape, dt))

        const = sb("const", [P, 2 * P])
        eps = sb("eps", [P, 1])
        x_sb = sb("x_sb", [P, TILES, C])
        mean_sb = sb("mean_sb", [P, TILES, 2])
        rstd = sb("rstd", [P, TILES])
        flag = sb("flag", [P, 1], I32)
        weight_all = sb("weight_all", [P, 2, TILES])
        tile_row = sb("tile_row", [1, MOE_TILES], I32)
        tile_expert = sb("tile_expert", [1, MOE_TILES], I32)
        rows_in = nc.dram_tensor("rows_in", (ROW_TILES * TR, CW), F32).ap()
        chosen_rows = nc.dram_tensor("chosen_rows", (NOWHERE + MOE_TILES * TR, C), F32).ap()
        agg_T = sb("agg_T", [P, TILES * P])
        neighbour_maxima(nc, x, adj_t, small, counting, const, eps, x_sb, mean_sb, rstd, agg_T, flag)
        general_maxima(nc, adj, priority, const, x_sb, mean_sb, rstd, agg_T, flag)
        m_all = sb("m_all", [P, TILES, C])
        w1_sb = sb("w1_sb", [P, E, F])
        w2_sb = sb("w2_sb", [P, E, FC * C])
        b1_sb = sb("b1_sb", [P, E, FC])
        b2_sb = sb("b2_sb", [P, E, C])
        expert_loads = (
            (w1_sb[:], w1.rearrange("e p f -> p e f")),
            (b1_sb[:], b1),
            (w2_sb[:].rearrange("p e (k c) -> p e k c", k=FC), w2.rearrange("e (k p) c -> p e k c", p=P)),
            (b2_sb[:].rearrange("p e c -> p (e c)"), b2.rearrange("e c -> (e c)").partition_broadcast(P)),
        )
        tokens(nc, W, b, gate_w, gate_b, moe_small, gate_consts, x_sb, mean_sb, rstd, agg_T, m_all,
               weight_all, tile_row, tile_expert, rows_in, const, eps, expert_loads)
        experts(nc, nowhere_rows, w1_sb, b1_sb, w2_sb, b2_sb, const, tile_row, tile_expert, rows_in, chosen_rows)
        results(nc, gamma, beta, out, x_sb, m_all, weight_all, chosen_rows, eps)
    return nc


def neighbour_maxima(nc, x, adj_t, small, counting, const, eps, x_sb, mean_sb, rstd, agg_T, flag):
    with ExitStack() as ctx:
        def sb(name, shape, dt=F32):
            return ctx.enter_context(nc.sbuf_tensor(name, shape, dt))

        def ps(name, shape):
            return ctx.enter_context(nc.psum_tensor(name, shape, F32))

        def sem(name):
            return ctx.enter_context(nc.semaphore(name))

        cnt = sb("cnt", [P, 4, P], F16)
        COUNT, CODE, ALL, LESS = (cnt[:, k, :] for k in range(4))
        beyond_s = sb("beyond_s", [P, 1])
        beyond_l = sb("beyond_l", [P, 1])
        ones_f = sb("ones_f", [P, P])
        nst = sb("nst", [P, BT, 6])
        nmv = sb("nmv", [P, BT, 2])
        std = sb("std", [P, TILES])
        n_scale = sb("n_scale", [P, TILES])
        n_shift = sb("n_shift", [P, TILES])
        n_next = sb("n_next", [P, BT, C])
        hi_next = sb("hi_next", [P, BT, C], F16)
        lo_next = sb("lo_next", [P, BT, C], F16)
        hi = sb("hi", [P, BT, C], F16)
        lo = sb("lo", [P, BT, C], F16)
        adj_sb = sb("adj_sb", [P, RUNS, GN], I32)
        edge = sb("edge", [P, RUNS, GN], F16)
        run_sum = sb("run_sum", [P, RUNS - 1, GN], F16)
        over = sb("over", [P, 2, GN], F16)
        code = sb("code", [P, 2, RUNS, GN], F16)
        rest = sb("rest", [P, RUNS, GN], F16)
        rest_code = sb("rest_code", [P, 2, RUNS, GN], F16)
        many = sb("many", [P, 2, GN], F16)
        mask = sb("mask", [P, MASK_RING, RUNS, GN], F16)
        best = sb("best", [P, 2, 2, GN])
        junk = sb("junk", [P, GN], F16)
        zero_flag = sb("zero_flag", [P, GROUPS])
        rest_flag = sb("rest_flag", [P, GROUPS])
        flags = sb("flags", [P, 2])

        rank_ps = [ps(f"rank_ps{k}", [P, GN]) for k in range(2)]
        unit_ps = [ps(f"unit_ps{k}", [P, 2, GN]) for k in range(RING)]

        small_in = sem("small_in")
        cnt_in = sem("cnt_in")
        x_in = [sem(f"x_in{k}") for k in range(2)]
        adj_in = sem("adj_in")
        pool_ready = sem("pool_ready")
        stat_steps = sem("stat_steps")
        var_ready = sem("var_ready")
        std_ready = sem("std_ready")
        scale_ready = sem("scale_ready")
        next_ready = sem("next_ready")
        next_steps = sem("next_steps")
        lo_ready = sem("lo_ready")
        parts_ready = sem("parts_ready")
        edge_ready = sem("edge_ready")
        edge_summed = sem("edge_summed")
        rest_ready = sem("rest_ready")
        rest_summed = sem("rest_summed")
        item_done = sem("item_done")
        item_read = sem("item_read")
        mask_ready = sem("mask_ready")
        unit_done = sem("unit_done")
        first_max = sem("first_max")
        unit_used = sem("unit_used")
        best_free = sem("best_free")
        best_merged = sem("best_merged")
        agg_ready = sem("agg_ready")
        flag_steps = sem("flag_steps")
        flags_summed = sem("flags_summed")

        NI = len(ITEMS)
        x_t = x.rearrange("b (t p) c -> p (b t) c", p=P)
        adj_g = adj_t.rearrange("q (k p) i -> q p k i", p=P)
        block = ctx.enter_context(nc.Block())

        @block.sync
        def _(sp):
            sp.dma_start(adj_sb[:], adj_g[0]).then_inc(adj_in, 16)
            sp.dma_start(cnt[:], counting).then_inc(cnt_in, 16)
            sp.dma_start(const[:], small).then_inc(small_in, 16)
            for k in range(4):
                tiles = slice(k * TILES // 4, (k + 1) * TILES // 4)
                sp.dma_start(x_sb[:, tiles, :], x_t[:, tiles, :]).then_inc(x_in[k // 2], 16)
            with sp.Fori(0, GROUPS - 1) as q:
                sp.wait_ge(edge_ready, q + 1)
                sp.dma_start(adj_sb[:], adj_g[q + 1]).then_inc(adj_in, 16)

        @block.gpsimd
        def _(pool):
            g = nc.gpsimd
            g.memset(eps[:], EPS).then_inc(pool_ready, 1)
            g.memset(beyond_s[:], -float(S)).then_inc(pool_ready, 1)
            g.memset(beyond_l[:], -float(L)).then_inc(pool_ready, 1)
            g.memset(ones_f[:], 1.0).then_inc(pool_ready, 1)

            def sums(q, src, ready, summed):
                dst = run_sum
                pool.wait_ge(ready, q + 1)
                for b in range(2, RUNS + 1):
                    if b > 2:
                        pool.wait_ge(summed, q * (RUNS - 1) + (b - 2))
                    before = src[:, 0, :] if b == 2 else dst[:, b - 3, :]
                    g.tensor_tensor(dst[:, b - 2, :], before, src[:, b - 1, :], ALU.add).then_inc(summed, 1)

            def low_part(gr):
                pool.wait_ge(next_ready, gr + 1)
                g.tensor_tensor(lo_next[:], n_next[:], hi_next[:], ALU.subtract).then_inc(lo_ready, 1)

            def prepare(q):
                if not (isinstance(q, int) and q == 0):
                    pool.wait_ge(item_done, q * NI)
                sums(q, edge, edge_ready, edge_summed)
                pool.wait_ge(item_done, q * NI + (AT["degree", 0] + 1))
                sums(q, rest, rest_ready, rest_summed)

            prepare(0)
            low_part(0)
            with pool.Fori(0, B - 1) as gr:
                prepare(gr * GB + 1)
                low_part(gr + 1)
                prepare(gr * GB + 2)
            prepare((B - 1) * GB + 1)

        def rank_item(pe, q, n):
            kind, b, bank = ITEMS[n]
            t = nc.tensor
            before_q = q - 1
            dst = rank_ps[bank][:]
            earlier = [k for k in range(n) if ITEMS[k][2] == bank]
            if earlier:
                pe.wait_ge(item_read, q * NI + (earlier[-1] + 1))
            elif not (isinstance(q, int) and q == 0):
                last = max(k for k in range(NI) if ITEMS[k][2] == bank)
                pe.wait_ge(item_read, q * NI + (last + 1 - NI))
            if kind == "all":
                if b == 0:
                    pe.wait_ge(edge_ready, q + 1)
                if b >= 2:
                    pe.wait_ge(edge_summed, q * (RUNS - 1) + (b - 1))
                ins = t.matmul(dst, COUNT, edge[:, b, :], start=True, stop=(b == 0))
                if b > 0:
                    ins = t.matmul(dst, ALL, edge[:, 0, :] if b == 1 else run_sum[:, b - 2, :],
                                   start=False, stop=True)
            elif kind == "run":
                t.matmul(dst, CODE, edge[:, b, :], start=True, stop=False)
                pe.wait_ge(item_read, q * NI + (AT["all", b] + 1))
                ins = t.matmul(dst, LESS, over[:, b % 2, :], start=False, stop=True)
            elif kind == "degree":
                pe.wait_ge(edge_summed, q * (RUNS - 1) + (RUNS - 1))
                ins = t.matmul(dst, ALL, run_sum[:, RUNS - 2, :], start=True, stop=True)
            elif kind == "rest":
                if b == 0:
                    pe.wait_ge(rest_ready, q + 1)
                if b >= 2:
                    pe.wait_ge(rest_summed, q * (RUNS - 1) + (b - 1))
                ins = t.matmul(dst, CODE, rest[:, b, :], start=True, stop=(b == 0))
                if b > 0:
                    ins = t.matmul(dst, ALL, rest[:, 0, :] if b == 1 else run_sum[:, b - 2, :],
                                   start=False, stop=True)
            else:
                pe.wait_ge(rest_summed, q * (RUNS - 1) + (RUNS - 1))
                ins = t.matmul(dst, ALL, run_sum[:, RUNS - 2, :], start=True, stop=True)
            ins.then_inc(item_done, 1)

        def slots_of(u):
            period, k = divmod(u, PU)
            if k == MIDDLE:
                return [(2 * period + 1, list(range(RUNS)))]
            b = 2 * (k if k < MIDDLE else k - 1)
            return [(2 * period, [b]), (2 * period, [b + 1])]

        def last_unit(k):
            return max(u for u in range(UNITS) if any(c == k for c, _ in slots_of(u)))

        @block.tensor
        def _(pe):
            t = nc.tensor
            pe.sem_inc(unit_done, UNITS)
            pe.wait_ge(cnt_in, 16)
            pe.wait_ge(pool_ready, 4)
            for n in range(NI):
                rank_item(pe, 0, n)

            def unit(q, gr, h, u):
                if u == 0 and h == 0:
                    pe.wait_ge(parts_ready, 2 * gr + 1)
                if u == MIDDLE and h == 0:
                    pe.wait_ge(parts_ready, 2 * gr + 2)
                same = [k for k in range(UNITS) if BANKS[k] == BANKS[u]]
                before = max(k + UNITS if k < u else k for k in same if k != u)
                pe.wait_ge(unit_used, q * UNITS + (before + 1))
                for s, (k, runs) in enumerate(slots_of(u)):
                    pe.wait_ge(mask_ready, q * MASKS + (k + 1))
                    for b in runs:
                        m = mask[:, k % MASK_RING, b, :]
                        dst = unit_ps[BANKS[u]][:, s, :]
                        t.matmul(dst, hi[:, b, :], m, start=(b == runs[0]), stop=False)
                        ins = t.matmul(dst, lo[:, b, :], m, start=False, stop=(b == runs[-1]))
                ins.then_inc(unit_done, 1)

            def group(q, gr, h, more):
                for u in range(UNITS):
                    unit(q, gr, h, u)
                    if more:
                        for n, (kind, b, _) in enumerate(ITEMS):
                            if BEHIND[kind, b] == u:
                                rank_item(pe, q + 1, n)

            with pe.Fori(0, B - 1) as gr:
                for h in range(GB):
                    group(gr * GB + h, gr, h, True)
            for h in range(GB):
                group((B - 1) * GB + h, B - 1, h, h == 0)
            pe.wait_ge(flag_steps, 2)
            t.matmul(rank_ps[0][:, 0:1], ones_f[:], flags[:, 0:1], start=True, stop=True).then_inc(flags_summed, 1)

        @block.scalar
        def _(act):
            s = nc.scalar
            act.wait_ge(pool_ready, 4)

            def item(q, h, n):
                kind, b, bank = ITEMS[n]
                src = rank_ps[bank][:]
                act.wait_ge(item_done, q * NI + (n + 1))
                if kind == "all":
                    ins = s.activation(over[:, b % 2, :], src, ACT.Relu, bias=beyond_s[:])
                elif kind == "run":
                    ins = s.copy(code[:, h, b, :], src)
                elif kind == "degree":
                    ins = s.activation(many[:, h, :], src, ACT.Relu, bias=beyond_s[:])
                elif kind == "rest":
                    ins = s.copy(rest_code[:, h, b, :], src)
                else:
                    column = slice(0, 1) if isinstance(q, int) and q == 0 else bass.ds(q, 1)
                    ins = s.activation(src, src, ACT.Relu, bias=beyond_l[:],
                                       accum_out=rest_flag[:, column])
                ins.then_inc(item_read, 1)

            def parts(gr):
                if not isinstance(gr, int):
                    act.wait_ge(parts_ready, 2 * gr)
                for t in range(BT):
                    col = bass.ds(gr * BT + t, 1)
                    ins = s.activation(n_next[:, t, :], x_sb[:, col, :], ACT.Identity,
                                       bias=n_shift[:, col], scale=n_scale[:, col])
                ins.then_inc(next_steps, 1)
                act.wait_ge(next_steps, gr + 1)
                s.copy(hi_next[:], n_next[:]).then_inc(next_ready, 1)

            def group(q, gr, h, more):
                ahead = [n for n, (kind, b, _) in enumerate(ITEMS) if BEHIND[kind, b] <= 1]
                if more:
                    for n in ahead:
                        item(q + 1, (h + 1) % 2, n)
                act.wait_ge(best_free, q + 1)
                act.wait_ge(unit_done, q * UNITS + (UNITS + 1))
                s.copy(best[:, 0, :, :], unit_ps[0][:]).then_inc(first_max, 1)
                if more:
                    for n in range(len(ahead), NI):
                        item(q + 1, (h + 1) % 2, n)

            for n in range(NI):
                item(0, 0, n)
            act.wait_ge(var_ready, 1)
            s.activation(std[:], mean_sb[:, :, 1], ACT.Sqrt, bias=eps[:]).then_inc(std_ready, 1)
            act.wait_ge(scale_ready, 1)
            parts(0)
            with act.Fori(0, B - 1) as gr:
                group(gr * GB, gr, 0, True)
                parts(gr + 1)
                group(gr * GB + 1, gr, 1, True)
            group((B - 1) * GB, B - 1, 0, True)
            group((B - 1) * GB + 1, B - 1, 1, False)

        @block.vector
        def _(dve):
            v = nc.vector

            def edges(q, half):
                if half == 0:
                    dve.wait_ge(adj_in, q * 16 + 16)
                runs = slice(half * RUNS // 2, (half + 1) * RUNS // 2)
                ins = v.tensor_scalar(edge[:, runs, :], adj_sb[:, runs, :], 0.0, None, ALU.not_equal)
                if half == 1:
                    ins.then_inc(edge_ready, 1)

            def rests(q, h):
                dve.wait_ge(item_read, q * NI + (AT["run", RUNS - 1] + 1))
                v.tensor_scalar(rest[:], code[:, h, :, :], HIT + R + 0.5, None,
                                ALU.is_gt).then_inc(rest_ready, 1)

            def statistics(first, last):
                with dve.Fori(first, last) as g:
                    dve.sem_clear(stat_steps)
                    for t in range(BT):
                        ins = v.bn_stats(nst[:, t, :], x_sb[:, bass.ds(g * BT + t, 1), :])
                    ins.then_inc(stat_steps, 1)
                    dve.wait_ge(stat_steps, 1)
                    for t in range(BT):
                        ins = v.bn_aggr(nmv[:, t, :], nst[:, t, :])
                    ins.then_inc(stat_steps, 1)
                    dve.wait_ge(stat_steps, 2)
                    v.tensor_copy(mean_sb[:, bass.ds(g * BT, BT), :], nmv[:]).then_inc(stat_steps, 1)
                    dve.wait_ge(stat_steps, 3)

            edges(0, 0)
            edges(0, 1)
            dve.wait_ge(x_in[0], 2 * 16)
            statistics(0, B // 2)
            rests(0, 0)
            dve.wait_ge(x_in[1], 2 * 16)
            statistics(B // 2, B)
            v.engine_nop().then_inc(var_ready, 1)
            dve.wait_ge(std_ready, 1)
            v.reciprocal(rstd[:], std[:]).then_inc(stat_steps, 1)
            dve.wait_ge(stat_steps, 4)
            v.tensor_scalar(n_scale[:], rstd[:], SCALE, None, ALU.mult).then_inc(stat_steps, 1)
            dve.wait_ge(stat_steps, 5)
            v.scalar_tensor_tensor(n_shift[:], mean_sb[:, :, 0], -1.0, n_scale[:], ALU.mult,
                                   ALU.mult).then_inc(scale_ready, 1)

            dve.sem_inc(unit_used, UNITS)
            dve.sem_inc(best_free, 1)

            def take_parts(runs):
                v.tensor_copy(hi[:, runs, :], hi_next[:, runs, :])
                v.tensor_copy(lo[:, runs, :], lo_next[:, runs, :]).then_inc(parts_ready, 1)

            def build_mask(q, h, k):
                old = k - MASK_RING
                if old >= 0:
                    dve.wait_ge(unit_done, q * UNITS + (UNITS + last_unit(old) + 1))
                else:
                    dve.wait_ge(unit_done, q * UNITS + (last_unit(old + MASKS) + 1))
                src, rank = (rest_code if k % 2 else code), k // 2 + 1
                if k == 0:
                    dve.wait_ge(item_read, q * NI + (AT["run", RUNS - 1] + 1))
                if k == 1:
                    dve.wait_ge(item_read, q * NI + NI)
                v.tensor_scalar(mask[:, k % MASK_RING, :, :], src[:, h, :, :], HIT + rank, None,
                                ALU.is_equal).then_inc(mask_ready, 1)

            def use(q, u):
                if u == 0:
                    dve.wait_ge(first_max, q + 1)
                    dve.sem_inc(unit_used, 1)
                    return
                dve.wait_ge(unit_done, q * UNITS + (UNITS + u + 1))
                if u == 1:
                    v.tensor_copy(best[:, 1, :, :], unit_ps[BANKS[u]][:]).then_inc(unit_used, 1)
                    return
                dve.wait_ge(unit_used, q * UNITS + (UNITS + u - 1))
                n = len(slots_of(u))
                mine = best[:, u % 2, 0:n, :]
                v.tensor_tensor(mine, unit_ps[BANKS[u]][:, 0:n, :], mine, ALU.max).then_inc(unit_used, 1)

            def group(q, gr, h, more, edges_too, next_graph):
                for u in range(UNITS):
                    period, k = divmod(u, PU)
                    if more and u == RUNS + 2:
                        rests(q + 1, (h + 1) % 2)
                    if k == MIDDLE and period < PERIODS - 1:
                        build_mask(q, h, 2 * period + 2)
                        build_mask(q, h, 2 * period + 3)
                    if k == MIDDLE and period == PERIODS - 1 and more:
                        build_mask(q + 1, (h + 1) % 2, 0)
                        build_mask(q + 1, (h + 1) % 2, 1)
                    if edges_too and u in EDGES_AT:
                        dve.wait_ge(item_done, q * NI + (NI + AT["degree", 0] + 1))
                        edges(q + 2, EDGES_AT.index(u))
                    if next_graph and u == UNITS - 1:
                        dve.wait_ge(lo_ready, gr + 2)
                        dve.wait_ge(unit_done, q * UNITS + (UNITS + (UNITS - PU + MIDDLE) + 1))
                        take_parts(slice(0, RUNS // 2))
                    use(q, u)
                if next_graph:
                    take_parts(slice(RUNS // 2, RUNS))
                dve.wait_ge(unit_used, q * UNITS + 2 * UNITS)
                columns = bass.ds(q * GN, GN)
                v.tensor_tensor(best[:, 0, :, :], best[:, 0, :, :], best[:, 1, :, :],
                                ALU.max).then_inc(best_merged, 1)
                dve.wait_ge(best_merged, q + 1)
                v.tensor_tensor(agg_T[:, columns], best[:, 0, 0, :], best[:, 0, 1, :],
                                ALU.max).then_inc(agg_ready, 1)
                dve.wait_ge(agg_ready, q + 1)
                dve.sem_inc(best_free, 1)
                v.scalar_tensor_tensor(junk[:], agg_T[:, columns], 0.0, many[:, h, :], ALU.is_equal,
                                       ALU.mult, accum_out=zero_flag[:, bass.ds(q, 1)])

            dve.wait_ge(lo_ready, 1)
            take_parts(slice(0, RUNS // 2))
            take_parts(slice(RUNS // 2, RUNS))
            build_mask(0, 0, 0)
            build_mask(0, 0, 1)
            dve.wait_ge(item_done, NI)
            edges(1, 0)
            edges(1, 1)
            with dve.Fori(0, B - 1) as gr:
                group(gr * GB, gr, 0, True, True, False)
                group(gr * GB + 1, gr, 1, True, True, True)
            group((B - 1) * GB, B - 1, 0, True, False, False)
            group((B - 1) * GB + 1, B - 1, 1, False, False, False)
            dve.drain()
            dve.wait_ge(item_read, GROUPS * NI)
            v.tensor_tensor(zero_flag[:], zero_flag[:], rest_flag[:], ALU.add).then_inc(flag_steps, 1)
            dve.wait_ge(flag_steps, 1)
            v.reduce_max(flags[:, 0:1], zero_flag[:], AX.X).then_inc(flag_steps, 1)
            dve.wait_ge(flags_summed, 1)
            v.tensor_scalar(flag[:], rank_ps[0][:, 0:1], 0.5, None, ALU.is_gt)


def general_maxima(nc, adj, priority, const, x_sb, mean_sb, rstd, agg_T, flag):
    with ExitStack() as ctx:
        def sb(name, shape, dt=F32):
            return ctx.enter_context(nc.sbuf_tensor(name, shape, dt))

        def sem(name):
            return ctx.enter_context(nc.semaphore(name))

        ident = const[:, 0:P]
        none_row = const[:, P + E:P + E + TILES]
        table = nc.dram_tensor("gather_table", (B, ROWS, C), F32).ap()
        table_b = table[:, 0:N, :].rearrange("b (t p) c -> b t p c", p=P)
        table_rows = table.rearrange("b r c -> (b r) c")
        adj_tiles = adj.rearrange("b (t p) j -> (b t) p j", p=P)

        pri = sb("pri", [P, N], F16)
        zrow = sb("zrow", [B, C])
        n_tile = sb("n_tile", [P, C])
        adj_tile = sb("adj_tile", [P, N], I32)
        score = sb("score", [P, N], F16)
        top = sb("top", [P, ROUNDS * TOP])
        nbr = sb("nbr", [P, S], I32)
        floor = sb("floor", [P, 1])
        got = sb("got", [P, S, C])
        most = sb("most", [P, C])
        tile_agg = sb("tile_agg", [P, C])
        turned = ctx.enter_context(nc.psum_tensor("gen_turned", [P, P], F32))

        pri_in = sem("pri_in")
        zero_made = sem("zero_made")
        table_out = sem("gen_table_out")
        n_made = sem("n_made")
        n_stored = sem("n_stored")
        tile_in = sem("tile_in")
        rank_steps = sem("gen_rank_steps")
        nbr_ready = sem("gen_nbr_ready")
        begun = sem("gen_begun")
        gathered = sem("gen_gathered")
        tile_ready = sem("tile_ready")
        tile_turned = sem("tile_turned")
        tile_done = sem("tile_done")
        block = ctx.enter_context(nc.Block())

        @block.sync
        def _(sp):
            wanted = sp.value_load(flag[0:1, 0:1], min_val=0, max_val=1)
            with sp.If(wanted > 0):
                sp.dma_start(pri[:], priority).then_inc(pri_in, 16)
                sp.wait_ge(zero_made, 1)
                sp.dma_start(table[:, N, :], zrow[:]).then_inc(table_out, 16)
                with sp.Fori(0, B) as g:
                    for t in range(BT):
                        sp.wait_ge(n_made, g * BT + (t + 1))
                        sp.dma_start(table_b[g, t], n_tile[:]).then_inc(n_stored, 16)
                sp.wait_ge(n_stored, 16 * (TILES + 1))
                sp.wait_ge(table_out, 16)
                sp.sem_inc(table_out, 1)
                sp.dma_start(adj_tile[:], adj_tiles[0]).then_inc(tile_in, 16)
                with sp.Fori(0, TILES - 1) as t:
                    sp.wait_ge(tile_done, t + 1)
                    sp.dma_start(adj_tile[:], adj_tiles[t + 1]).then_inc(tile_in, 16)

        @block.gpsimd
        def _(pool):
            wanted = pool.value_load(flag[0:1, 0:1], min_val=0, max_val=1)
            with pool.If(wanted > 0):
                pool.memset(zrow[:], 0.0).then_inc(zero_made, 1)
                pool.wait_ge(table_out, 17)
                with pool.Fori(0, TILES) as t:
                    pool.wait_ge(nbr_ready, t + 1)
                    pool.sem_inc(begun, 1)
                    for k in range(S):
                        pool.indirect_dma_start(
                            out=got[:, k, :], out_offset=None, in_=table_rows,
                            in_offset=bass.IndirectOffsetOnAxis(ap=nbr[:, k:k + 1], axis=0),
                        ).then_inc(gathered, 16)

        @block.tensor
        def _(pe):
            wanted = pe.value_load(flag[0:1, 0:1], min_val=0, max_val=1)
            with pe.If(wanted > 0):
                with pe.Fori(0, TILES) as t:
                    pe.wait_ge(tile_ready, t + 1)
                    nc.tensor.transpose(turned[:], tile_agg[:], ident).then_inc(tile_turned, 1)

        @block.vector
        def _(dve):
            v = nc.vector
            wanted = dve.value_load(flag[0:1, 0:1], min_val=0, max_val=1)
            with dve.If(wanted > 0):
                dve.sem_inc(n_stored, 16)
                with dve.Fori(0, TILES) as t:
                    tile = bass.ds(t, 1)
                    dve.wait_ge(n_stored, t * 16 + 16)
                    v.tensor_scalar(n_tile[:], x_sb[:, tile, :].rearrange("p a c -> p (a c)"),
                                    mean_sb[:, tile, 0], rstd[:, tile], ALU.subtract,
                                    ALU.mult).then_inc(n_made, 1)
                dve.wait_ge(pri_in, 16)
                with dve.Fori(0, TILES) as t:
                    steps = [0]

                    def after(instruction):
                        steps[0] += 1
                        instruction.then_inc(rank_steps, 1)
                        dve.wait_ge(rank_steps, steps[0])
                    dve.sem_clear(rank_steps)
                    dve.wait_ge(tile_in, t * 16 + 16)
                    after(v.scalar_tensor_tensor(score[:], adj_tile[:], 0.0, pri[:], ALU.not_equal, ALU.mult))
                    for r in range(ROUNDS):
                        eight = top[:, r * TOP:(r + 1) * TOP]
                        after(v.max(eight, score[:]))
                        if r < ROUNDS - 1:
                            after(v.match_replace(score[:], eight, score[:], 0.0))
                    v.tensor_scalar(nbr[:], top[:, 0:S], -1.0, none_row[:, bass.ds(t, 1)],
                                    ALU.mult, ALU.add).then_inc(nbr_ready, 1)
                    after(v.tensor_scalar(floor[:], top[:, S:S + 1], 0.5, LOWEST, ALU.is_gt, ALU.mult))
                    dve.wait_ge(gathered, t * (16 * S) + 16 * S)
                    after(v.tensor_reduce(most[:], got[:].rearrange("p k c -> p c k"), AX.X, ALU.max))
                    after(v.tensor_scalar(most[:], most[:], floor[:], None, ALU.max))
                    v.tensor_scalar(tile_agg[:], most[:], SCALE, None, ALU.mult).then_inc(tile_ready, 1)
                    dve.wait_ge(tile_turned, t + 1)
                    v.tensor_copy(agg_T[:, bass.ds(t * P, P)], turned[:]).then_inc(tile_done, 1)
                    dve.wait_ge(tile_done, t + 1)


def tokens(nc, W, b, gate_w, gate_b, moe_small, gate_consts, x_sb, mean_sb, rstd, agg_T, m_all,
           weight_all, tile_row, tile_expert, rows_in, const, eps, expert_loads):
    with ExitStack() as ctx:
        def sb(name, shape, dt=F32):
            return ctx.enter_context(nc.sbuf_tensor(name, shape, dt))

        def ps(name, shape, dt=F32):
            return ctx.enter_context(nc.psum_tensor(name, shape, dt))

        def sem(name):
            return ctx.enter_context(nc.semaphore(name))

        ident = const[:, 0:P]
        expert_ids = const[:, P:P + E]
        W_sb = sb("W_sb", [P, 2, C])
        rows = sb("rows", [1, C + E])
        ones = sb("ones", [1, P])
        gw_sb = sb("gw_sb", [P, E])
        grid = sb("grid", [P, GRID_COLS])
        earlier = sb("earlier", [P, 2, P], F16)
        EARLIER, ALL = earlier[:, 0, :], earlier[:, 1, :]
        queue_start = grid[:, 0:GT * E].rearrange("p (a e) -> p a e", a=GT)
        row_numbers = grid[:, GT * E:GT * E + 2 * TILES]
        number = grid[0:1, GT * E + 2 * TILES:]
        nobody = sb("nobody", [P, HALVES, CW])

        n_grp = sb("n_grp", [P, 2, GT, C])
        nT = sb("nT", [P, 2, GT, P])
        aggT = sb("aggT", [P, 2, GT, P])
        st = sb("st", [P, GT, 6])
        mv = sb("mv", [P, 2, GT, 2])
        sd = sb("sd", [P, 2, GT])
        rs = sb("rs", [P, GT])
        m = sb("m", [P, 2, GT, C])
        mT = sb("mT", [P, 2, GT, P])
        logit = sb("logit", [P, GT, E])
        top2 = sb("top2", [P, 2, GT, TOP])
        pick = sb("pick", [P, GT, TOP], U32)
        pickf = sb("pickf", [P, 2, GT])
        gap = sb("gap", [P, TILES])
        eg = sb("eg", [P, TILES])
        den = sb("den", [P, TILES])
        send = sb("send", [P, 2, 2, GT, CW])
        chosen = sb("chosen", [P, 2 * TILES, E], F16)
        placef = sb("placef", [P, 2 * GT])
        both = sb("both", [P, 2, GT, E], F16)
        group_sum = sb("group_sum", [P, E], F16)
        run = sb("run", [P, GROUPS + 1, E], F16)
        place = sb("place", [P, GT, E])
        picked = sb("picked", [P, 2, GT, E])
        slot = sb("slot", [P, 2, 2 * GT], I32)
        count = sb("count", [P, E])
        tail = sb("tail", [1, E], I32)
        row = {k: sb(f"row_{k}", [P, E]) for k in ("tiles", "ones", "upto")}
        row_int = sb("row_int", [P, E], I32)
        past = sb("past", [1, MOE_TILES, E])
        line = {k: sb(f"line_{k}", [1, MOE_TILES]) for k in ("expert", "before", "index", "row")}

        turned = ps("turned", [P, GT, P])
        lin = [ps(f"lin{k}", [P, GT, C]) for k in range(2)]
        m_turned_ps = ps("m_turned_ps", [P, GT, P])
        logit_ps = [ps(f"logit_ps{k}", [P, GT, E]) for k in range(2)]
        place_ps = [ps(f"place_ps{k}", [P, GT, E]) for k in range(2)]

        consts_in = sem("consts_in")
        pool_ready = sem("tok_pool_ready")
        spare_out = sem("spare_out")
        weights_in = sem("weights_in")
        n_taken = sem("n_taken")
        nT_turned = sem("nT_turned")
        nT_ready = sem("nT_ready")
        aggT_ready = sem("aggT_ready")
        lin_ready = sem("lin_ready")
        x1_steps = sem("x1_steps")
        x1_stats = sem("x1_stats")
        x1_std = sem("x1_std")
        m_steps = sem("m_steps")
        m_ready = sem("m_ready")
        m_kept = sem("m_kept")
        m_turned = sem("m_turned")
        mT_ready = sem("mT_ready")
        logit_ready = sem("logit_ready")
        pick_steps = sem("pick_steps")
        gap_ready = sem("gap_ready")
        exp_ready = sem("exp_ready")
        sent_ready = sem("sent_ready")
        both_ready = sem("both_ready")
        run_ready = sem("run_ready")
        place_ready = sem("place_ready")
        place_steps = sem("place_steps")
        slot_ready = sem("slot_ready")
        begun = sem("scatters_begun")
        scattered = [sem(f"scattered{k}") for k in range(2)]
        counted = sem("counted")
        tail_ready = sem("tail_ready")
        tails_out = sem("tails_out")
        list_steps = sem("list_steps")

        block = ctx.enter_context(nc.Block())
        CONST_LOADS = 6

        def clear_tails(engine, first):
            engine.wait_ge(pool_ready, 3)
            engine.wait_ge(tail_ready, 1)
            for e in range(first, E, 2):
                start = engine.value_load(tail[0:1, e:e + 1], min_val=0, max_val=E * QUEUE - TR)
                engine.dma_start(rows_in[bass.ds(start, TR), :].rearrange("(p u) c -> p u c", p=P),
                                 nobody[:]).then_inc(tails_out, 16)

        @block.sync
        def _(sp):
            for dst, src in (
                (W_sb[:], W.rearrange("(k p) o -> p k o", p=P)),
                (rows[:, 0:C], b.rearrange("(a c) -> a c", a=1)),
                (rows[:, C:C + E], gate_b.rearrange("(a c) -> a c", a=1)),
                (gw_sb[:], gate_w),
                (grid[:], moe_small),
                (earlier[:], gate_consts),
            ):
                sp.dma_start(dst, src).then_inc(consts_in, 16)
            sp.wait_ge(pool_ready, 3)
            spare = rows_in[E * QUEUE:, :].rearrange("(p u) c -> p u c", p=P)
            sp.dma_start(spare, nobody[:]).then_inc(spare_out, 16)
            for dst, src in expert_loads:
                sp.dma_start(dst, src).then_inc(weights_in, 16)
            sp.wait_ge(spare_out, 16)
            sp.wait_ge(weights_in, 16 * len(expert_loads))
            clear_tails(sp, 0)
            sp.wait_ge(tails_out, 16 * E)

        LAGS = 6

        def stages(engine, step):
            for j in range(LAGS + 2):
                step(0, j)
            with engine.Fori(LAGS // 2 + 1, GROUPS // 2) as it:
                step(it, 0)
                step(it, 1)
            for j in range(LAGS):
                step(GROUPS // 2, j)

        def exists(it, k, lag):
            if not isinstance(it, int):
                return True
            return 0 <= 2 * it + k - lag < GROUPS

        def place_of(it, k, lag):
            return it * 2 + (k - lag), (k - lag) % 2, it + (k - lag) // 2

        @block.gpsimd
        def _(pool):
            g = nc.gpsimd
            g.memset(ones[:], 1.0).then_inc(pool_ready, 1)
            g.memset(nobody[:], 0.0).then_inc(pool_ready, 1)
            pool.wait_ge(pool_ready, 2)
            g.memset(nobody[:, :, C:CW], NOBODY).then_inc(pool_ready, 1)

            def step(it, k):
                if not exists(it, k, 5):
                    return
                i, h, _ = place_of(it, k, 5)
                pool.wait_ge(sent_ready, i + 1)
                pool.wait_ge(slot_ready, i + 1)
                pool.sem_inc(begun, 1)
                for c in range(2):
                    for a in range(GT):
                        col = slice(c * GT + a, c * GT + a + 1)
                        pool.indirect_dma_start(
                            out=rows_in, in_=send[:, h, c, a, :], in_offset=None,
                            out_offset=bass.IndirectOffsetOnAxis(ap=slot[:, h, col], axis=0),
                        ).then_inc(scattered[h], 16)
            stages(pool, step)
            for h in range(2):
                pool.wait_ge(scattered[h], 16 * 2 * GT * (GROUPS // 2))

        @block.vector
        def _(dve):
            v = nc.vector

            def stage_n(it, k):
                i, h, _ = place_of(it, k, 0)
                if not (isinstance(i, int) and i < 2):
                    dve.wait_ge(nT_turned, i - 1)
                for a in range(GT):
                    col = bass.ds(i * GT + a, 1)
                    ins = v.tensor_scalar(n_grp[:, h, a, :], x_sb[:, col, :], mean_sb[:, col, 0], rstd[:, col],
                                          ALU.subtract, ALU.mult)
                ins.then_inc(n_taken, 1)

            def stage_x1(it, k):
                i, h, _ = place_of(it, k, 2)
                tiles = bass.ds(i * GT, GT)
                dve.sem_clear(x1_steps)
                dve.wait_ge(lin_ready, i + 1)
                v.scalar_tensor_tensor(x_sb[:, tiles, :], lin[h][:], 0.0, x_sb[:, tiles, :], ALU.max,
                                       ALU.add).then_inc(x1_steps, 1)
                dve.wait_ge(x1_steps, 1)
                for a in range(GT):
                    ins = v.bn_stats(st[:, a, :], x_sb[:, bass.ds(i * GT + a, 1), :])
                ins.then_inc(x1_steps, 1)
                dve.wait_ge(x1_steps, 2)
                for a in range(GT):
                    ins = v.bn_aggr(mv[:, h, a, :], st[:, a, :])
                ins.then_inc(x1_stats, 1)

            def stage_m(it, k):
                i, h, half = place_of(it, k, 2)
                dve.sem_clear(m_steps)
                dve.wait_ge(x1_std, i + 1)
                v.reciprocal(rs[:], sd[:, h, :]).then_inc(m_steps, 1)
                if not (isinstance(i, int) and i < 2):
                    dve.wait_ge(m_turned, i - 1)
                    dve.wait_ge(m_kept, i - 1)
                dve.wait_ge(m_steps, 1)
                for a in range(GT):
                    ins = v.tensor_scalar(m[:, h, a, :], x_sb[:, bass.ds(i * GT + a, 1), :], mv[:, h, a, 0:1],
                                          rs[:, a:a + 1], ALU.subtract, ALU.mult)
                ins.then_inc(m_ready, 1)

            def stage_top(it, k):
                i, h, _ = place_of(it, k, 4)
                dve.sem_clear(pick_steps)
                dve.wait_ge(logit_ready, i + 1)
                v.tensor_copy(logit[:], logit_ps[h][:]).then_inc(pick_steps, 1)
                dve.wait_ge(pick_steps, 1)
                for a in range(GT):
                    ins = v.max(top2[:, h, a, :], logit[:, a, :])
                ins.then_inc(pick_steps, 1)
                dve.wait_ge(pick_steps, 2)
                v.tensor_tensor(gap[:, bass.ds(i * GT, GT)], top2[:, h, :, 1], top2[:, h, :, 0],
                                ALU.subtract).then_inc(gap_ready, 1)
                for a in range(GT):
                    ins = v.max_index(pick[:, a, :], top2[:, h, a, :], logit[:, a, :])
                ins.then_inc(pick_steps, 1)
                dve.wait_ge(pick_steps, 3)
                v.tensor_copy(pickf[:], pick[:, :, 0:2].rearrange("p a c -> p c a")).then_inc(pick_steps, 1)

            def stage_pick(it, k):
                i, h, _ = place_of(it, k, 4)
                dve.wait_ge(pick_steps, 4)
                for c in range(2):
                    v.tensor_tensor(chosen[:, bass.ds(i * (2 * GT) + c * GT, GT), :],
                                    expert_ids.unsqueeze(1).to_broadcast([P, GT, E]),
                                    pickf[:, c, :].unsqueeze(2).to_broadcast([P, GT, E]),
                                    ALU.is_equal).then_inc(pick_steps, 1)
                if not (isinstance(i, int) and i < 2):
                    dve.wait_ge(place_ready, i - 1)
                dve.wait_ge(pick_steps, 6)
                v.tensor_tensor(both[:, h, :, :], chosen[:, bass.ds(i * (2 * GT), GT), :],
                                chosen[:, bass.ds(i * (2 * GT) + GT, GT), :], ALU.add).then_inc(both_ready, 1)
                dve.wait_ge(both_ready, i + 1)
                dve.wait_ge(run_ready, i + 1)
                with nc.allow_low_precision(reason="counts up to 128 are exact"):
                    v.tensor_reduce(group_sum[:], both[:, h, :, :].rearrange("p a e -> p e a"), AX.X,
                                    ALU.add).then_inc(pick_steps, 1)
                dve.wait_ge(pick_steps, 7)
                v.tensor_tensor(run[:, bass.ds(i + 1, 1), :], run[:, bass.ds(i, 1), :],
                                group_sum[:].unsqueeze(1), ALU.add).then_inc(run_ready, 1)

            def stage_place(it, k):
                i, h, half = place_of(it, k, 5)
                these = bass.ds(i * (2 * GT), 2 * GT)
                dve.sem_clear(place_steps)
                if not (isinstance(i, int) and i < 2):
                    dve.wait_ge(scattered[h], half * (16 * 2 * GT))
                dve.wait_ge(place_ready, i + 1)
                v.tensor_tensor(place[:], place_ps[h][:], queue_start, ALU.add).then_inc(place_steps, 1)
                dve.wait_ge(place_steps, 1)
                v.tensor_tensor(picked[:].rearrange("p c a e -> p c (a e)"),
                                chosen[:, these, :].rearrange("p (c a) e -> p c (a e)", c=2),
                                place[:].rearrange("p a e -> p (a e)").unsqueeze(1).to_broadcast([P, 2, GT * E]),
                                ALU.mult).then_inc(place_steps, 1)
                dve.wait_ge(place_steps, 2)
                v.tensor_reduce(placef[:], picked[:].rearrange("p c a e -> p (c a) e"), AX.X,
                                ALU.add).then_inc(place_steps, 1)
                dve.wait_ge(place_steps, 3)
                v.tensor_copy(slot[:, h, :], placef[:]).then_inc(slot_ready, 1)

            def step(it, k):
                if exists(it, k, 2):
                    stage_x1(it, k)
                if exists(it, k, 5):
                    stage_place(it, k)
                if exists(it, k, 4):
                    stage_top(it, k)
                if exists(it, k, 0):
                    stage_n(it, k)
                if exists(it, k, 4):
                    stage_pick(it, k)
                if exists(it, k, 2):
                    stage_m(it, k)

            v.memset(run[:, 0, :], 0.0).then_inc(run_ready, 1)
            v.memset(row["ones"][:], 1.0).then_inc(list_steps, 1)
            dve.wait_ge(consts_in, 16 * CONST_LOADS)
            stages(dve, step)

            dve.wait_ge(counted, 1)
            v.tensor_copy(count[:], place_ps[0][:, 0, :]).then_inc(list_steps, 1)
            dve.wait_ge(list_steps, 2)
            n = 2

            def after(instruction):
                nonlocal n
                n += 1
                instruction.then_inc(list_steps, 1)
                dve.wait_ge(list_steps, n)
            v.tensor_tensor(tail[:], count[0:1, :], queue_start[0:1, 0, :], ALU.add).then_inc(tail_ready, 1)

            after(v.tensor_scalar(row_int[:], count[:], float(TR - 1), None, ALU.add))
            after(v.tensor_scalar(row_int[:], row_int[:], TR.bit_length() - 1, None, ALU.arith_shift_right))
            after(v.tensor_copy(row["tiles"][:], row_int[:]))
            after(v.tensor_tensor_scan(row["upto"][:], row["ones"][:], row["tiles"][:], 0.0, ALU.mult, ALU.add))
            wide = [1, MOE_TILES, E]
            after(v.tensor_tensor(past[:], number.unsqueeze(2).to_broadcast(wide),
                                  row["upto"][0:1, :].unsqueeze(1).to_broadcast(wide), ALU.is_ge))
            after(v.tensor_reduce(line["expert"][:], past[:], AX.X, ALU.add))
            after(v.tensor_tensor(past[:], past[:], row["tiles"][0:1, :].unsqueeze(1).to_broadcast(wide), ALU.mult))
            after(v.tensor_reduce(line["before"][:], past[:], AX.X, ALU.add))
            after(v.tensor_tensor(line["index"][:], number, line["before"][:], ALU.subtract))
            after(v.tensor_scalar(line["row"][:], line["expert"][:], float(QUEUE // TR), None, ALU.mult))
            after(v.tensor_tensor(line["row"][:], line["row"][:], line["index"][:], ALU.add))
            after(v.tensor_scalar(tile_row[:], line["row"][:], float(ROW_TILES - 1), None, ALU.min))
            after(v.tensor_scalar(tile_expert[:], line["expert"][:], float(E - 1), None, ALU.min))
            dve.wait_ge(exp_ready, 1)
            after(v.tensor_scalar(den[:], eg[:], 1.0, None, ALU.add))
            after(v.reciprocal(weight_all[:, 0, :], den[:]))
            after(v.tensor_tensor(weight_all[:, 1, :], eg[:], weight_all[:, 0, :], ALU.mult))

        @block.scalar
        def _(act):
            s = nc.scalar

            def step(it, k):
                if exists(it, k, 1):
                    i, h, _ = place_of(it, k, 1)
                    if not (isinstance(i, int) and i < 2):
                        act.wait_ge(lin_ready, i - 1)
                    s.activation(aggT[:, h, :, :], agg_T[:, bass.ds(i * GN, GN)].rearrange("p (a q) -> p a q", a=GT),
                                 ACT.Copy, scale=1.0 / SCALE).then_inc(aggT_ready, 1)
                    act.wait_ge(nT_turned, i + 1)
                    s.copy(nT[:, h, :, :], turned[:]).then_inc(nT_ready, 1)
                if exists(it, k, 3):
                    i, h, _ = place_of(it, k, 3)
                    if not (isinstance(i, int) and i < 2):
                        act.wait_ge(logit_ready, i - 1)
                    act.wait_ge(m_turned, i + 1)
                    s.copy(mT[:, h, :, :], m_turned_ps[:]).then_inc(mT_ready, 1)
                if exists(it, k, 2):
                    i, h, _ = place_of(it, k, 2)
                    act.wait_ge(x1_stats, i + 1)
                    s.activation(sd[:, h, :], mv[:, h, :, 1], ACT.Sqrt, bias=eps[:]).then_inc(x1_std, 1)
                if exists(it, k, 3):
                    i, h, _ = place_of(it, k, 3)
                    act.wait_ge(m_ready, i + 1)
                    s.copy(m_all[:, bass.ds(i * GT, GT), :], m[:, h, :, :]).then_inc(m_kept, 1)
                if exists(it, k, 5):
                    i, h, half = place_of(it, k, 5)
                    act.wait_ge(m_kept, i + 1)
                    if not (isinstance(i, int) and i < 2):
                        act.wait_ge(scattered[h], half * (16 * 2 * GT))
                    for c in range(2):
                        s.copy(send[:, h, c, :, 0:C], m_all[:, bass.ds(i * GT, GT), :])
                    s.copy(send[:, h, :, :, C],
                           row_numbers[:, bass.ds(i * (2 * GT), 2 * GT)].rearrange("p (c a) -> p c a", c=2)).then_inc(sent_ready, 1)
            stages(act, step)
            act.wait_ge(gap_ready, GROUPS)
            s.activation(eg[:], gap[:], ACT.Exp).then_inc(exp_ready, 1)
            clear_tails(act, 1)

        @block.tensor
        def _(pe):
            t = nc.tensor

            def step(it, k):
                if exists(it, k, 1):
                    i, h, _ = place_of(it, k, 1)
                    if not (isinstance(i, int) and i < 1):
                        pe.wait_ge(nT_ready, i)
                    pe.wait_ge(n_taken, i + 1)
                    for a in range(GT):
                        ins = t.transpose(turned[:, a, :], n_grp[:, h, a, :], ident)
                    ins.then_inc(nT_turned, 1)
                if exists(it, k, 3):
                    i, h, _ = place_of(it, k, 3)
                    if not (isinstance(i, int) and i < 1):
                        pe.wait_ge(mT_ready, i)
                    pe.wait_ge(m_ready, i + 1)
                    for a in range(GT):
                        ins = t.transpose(m_turned_ps[:, a, :], m[:, h, a, :], ident)
                    ins.then_inc(m_turned, 1)
                if exists(it, k, 1):
                    i, h, _ = place_of(it, k, 1)
                    if not (isinstance(i, int) and i < 2):
                        pe.wait_ge(x1_stats, i - 1)
                    pe.wait_ge(aggT_ready, i + 1)
                    pe.wait_ge(nT_ready, i + 1)
                    for a in range(GT):
                        t.matmul(lin[h][:, a, :], nT[:, h, a, :], W_sb[:, 0, :], start=True, stop=False)
                        t.matmul(lin[h][:, a, :], aggT[:, h, a, :], W_sb[:, 1, :], start=False, stop=False)
                        ins = t.matmul(lin[h][:, a, :], ones[:], rows[:, 0:C], start=False, stop=True)
                    ins.then_inc(lin_ready, 1)
                if exists(it, k, 3):
                    i, h, _ = place_of(it, k, 3)
                    if not (isinstance(i, int) and i < 2):
                        pe.wait_ge(gap_ready, i - 1)
                    pe.wait_ge(mT_ready, i + 1)
                    for a in range(GT):
                        t.matmul(logit_ps[h][:, a, :], mT[:, h, a, :], gw_sb[:], start=True, stop=False)
                        ins = t.matmul(logit_ps[h][:, a, :], ones[:], rows[:, C:C + E],
                                       start=False, stop=True)
                    ins.then_inc(logit_ready, 1)
                if exists(it, k, 4):
                    i, h, _ = place_of(it, k, 4)
                    if not (isinstance(i, int) and i < 2):
                        pe.wait_ge(slot_ready, i - 1)
                    pe.wait_ge(both_ready, i + 1)
                    pe.wait_ge(run_ready, i + 1)
                    for a in range(GT):
                        dst = place_ps[h][:, a, :]
                        t.matmul(dst, EARLIER, both[:, h, a, :], start=True, stop=False)
                        for c in range(a):
                            t.matmul(dst, ALL, both[:, h, c, :], start=False, stop=False)
                        ins = t.matmul(dst, ALL, run[:, bass.ds(i, 1), :].rearrange("p a e -> p (a e)"),
                                       start=False, stop=True)
                    ins.then_inc(place_ready, 1)
            pe.wait_ge(consts_in, 16 * CONST_LOADS)
            pe.wait_ge(pool_ready, 2)
            stages(pe, step)
            pe.wait_ge(run_ready, GROUPS + 1)
            pe.wait_ge(slot_ready, GROUPS)
            t.matmul(place_ps[0][:, 0, :], ALL, run[:, GROUPS, :], start=True, stop=True).then_inc(counted, 1)


def experts(nc, nowhere_rows, w1_sb, b1_sb, w2_sb, b2_sb, const, tile_row, tile_expert, rows_in, chosen_rows):
    with ExitStack() as ctx:
        def sb(name, shape, dt=F32):
            return ctx.enter_context(nc.sbuf_tensor(name, shape, dt))

        def ps(name, shape):
            return ctx.enter_context(nc.psum_tensor(name, shape, F32))

        def sem(name):
            return ctx.enter_context(nc.semaphore(name))

        ident = const[:, 0:P]
        x_in = sb("x_in", [P, SLOTS, HALVES, CW])
        nowhere = sb("nowhere", [P, MOE_TILES, HALVES])
        target = sb("target", [P, SLOTS, HALVES], I32)
        xT = sb("xT", [P, 2, HALVES, P])
        w1_at = sb("w1_at", [P, 2, F])
        hT = sb("hT", [P, 2, FC, HALVES * P])
        o_sb = sb("o_sb", [P, SLOTS, HALVES, C])
        xT_ps = [ps(f"xT_ps{k}", [P, HALVES, P]) for k in range(2)]
        h_ps = [ps(f"h_ps{k}", [P, FC, HALVES * P]) for k in range(2)]
        o_ps = [ps(f"o_ps{k}", [P, HALVES, C]) for k in range(2)]

        loaded = [sem(f"loaded{k}") for k in range(SLOTS)]
        stored = [sem(f"stored{k}") for k in range(SLOTS)]
        x_turned = sem("x_turned")
        xT_ready = sem("xT_ready")
        inner_ready = sem("inner_ready")
        w1_ready = sem("w1_ready")
        relu_ready = sem("relu_ready")
        outer_ready = sem("outer_ready")
        nowhere_in = sem("nowhere_in")
        target_ready = sem("target_ready")
        o_ready = sem("o_ready")
        begun = sem("stores_begun")

        tiles_in = rows_in.rearrange("(t p u) c -> t p u c", p=P, u=HALVES)
        block = ctx.enter_context(nc.Block())
        LAST = 2

        def stages(engine, step):
            for k in range(2 * SLOTS):
                step(0, k)
            with engine.Fori(2, MOE_TILES // SLOTS) as it:
                for k in range(SLOTS):
                    step(it, k)
            for k in range(LAST):
                step(MOE_TILES // SLOTS, k)

        def tile_of(it, k, lag):
            if isinstance(it, int) and not 0 <= SLOTS * it + k - lag < MOE_TILES:
                return None
            return it * SLOTS + (k - lag)

        def at(tile):
            return slice(tile, tile + 1) if isinstance(tile, int) else bass.ds(tile, 1)

        def expert_of(engine, tile):
            return engine.value_load(tile_expert[0:1, at(tile)], min_val=0, max_val=E - 1)

        def row_of(engine, tile):
            return engine.value_load(tile_row[0:1, at(tile)], min_val=0, max_val=ROW_TILES - 1)

        @block.sync
        def _(sp):
            def load(it, k, lag):
                tile = tile_of(it, k, lag)
                if tile is None:
                    return
                slot = (k - lag) % SLOTS
                row = row_of(sp, tile)
                if not (isinstance(tile, int) and tile < SLOTS):
                    sp.wait_ge(target_ready, tile - SLOTS + 1)
                sp.dma_start(x_in[:, slot, :, :], tiles_in[row]).then_inc(loaded[slot], 16)

            sp.dma_start(nowhere[:], nowhere_rows).then_inc(nowhere_in, 16)
            for tile in range(AHEAD):
                load(0, tile, 0)
            for j in range(SLOTS):
                load(0, j, -AHEAD)
            with sp.Fori(1, MOE_TILES // SLOTS - 1) as it:
                for k in range(SLOTS):
                    load(it, k, -AHEAD)
            for k in range(SLOTS):
                load(MOE_TILES // SLOTS - 1, k, -AHEAD)

        @block.gpsimd
        def _(pool):
            def step(it, k):
                if (tile := tile_of(it, k, LAST)) is not None:
                    slot = (k - LAST) % SLOTS
                    pool.wait_ge(o_ready, tile + 1)
                    pool.sem_inc(begun, 1)
                    for u in range(HALVES):
                        pool.indirect_dma_start(
                            out=chosen_rows, in_=o_sb[:, slot, u, :], in_offset=None,
                            out_offset=bass.IndirectOffsetOnAxis(ap=target[:, slot, u:u + 1], axis=0),
                        ).then_inc(stored[slot], 16)
            stages(pool, step)
            for k in range(SLOTS):
                pool.wait_ge(stored[k], 16 * HALVES * (MOE_TILES // SLOTS))

        @block.tensor
        def _(pe):
            t = nc.tensor

            def step(it, k):
                if (tile := tile_of(it, k, 0)) is not None:
                    slot = k % SLOTS
                    pe.wait_ge(loaded[slot], it * 16 + (16 * (k // SLOTS) + 16))
                    for u in range(HALVES):
                        ins = t.transpose(xT_ps[k % 2][:, u, :], x_in[:, slot, u, 0:C], ident)
                    ins.then_inc(x_turned, 1)
                if (tile := tile_of(it, k, 1)) is not None:
                    par = (k - 1) % 2
                    pe.wait_ge(xT_ready, tile + 1)
                    pe.wait_ge(w1_ready, tile + 1)
                    for f in range(FC):
                        ins = t.matmul(h_ps[par][:, f, :], w1_at[:, par, f * P:(f + 1) * P],
                                       xT[:, par, :, :].rearrange("p u q -> p (u q)"), start=True, stop=True)
                    ins.then_inc(inner_ready, 1)
                if (tile := tile_of(it, k, 2)) is not None:
                    par = (k - 2) % 2
                    e = expert_of(pe, tile)
                    if not (isinstance(tile, int) and tile < 2):
                        pe.wait_ge(o_ready, tile - 1)
                    pe.wait_ge(relu_ready, tile + 1)
                    for u in range(HALVES):
                        for f in range(FC):
                            w = w2_sb[:, bass.ds(e, 1), f * C:(f + 1) * C].rearrange("p a c -> p (a c)")
                            ins = t.matmul(o_ps[par][:, u, :], hT[:, par, f, u * P:(u + 1) * P], w,
                                           start=(f == 0), stop=(f == FC - 1))
                    ins.then_inc(outer_ready, 1)
            stages(pe, step)

        @block.scalar
        def _(act):
            s = nc.scalar

            def step(it, k):
                if (tile := tile_of(it, k, 0)) is not None:
                    act.wait_ge(x_turned, tile + 1)
                    s.copy(xT[:, k % 2, :, :], xT_ps[k % 2][:]).then_inc(xT_ready, 1)
                if (tile := tile_of(it, k, 1)) is not None:
                    par = (k - 1) % 2
                    e = expert_of(act, tile)
                    act.wait_ge(inner_ready, tile + 1)
                    for f in range(FC):
                        ins = s.activation(hT[:, par, f, :], h_ps[par][:, f, :], ACT.Relu,
                                           bias=b1_sb[:, bass.ds(e, 1), f])
                    ins.then_inc(relu_ready, 1)
            stages(act, step)

        @block.vector
        def _(dve):
            v = nc.vector

            def step(it, k):
                if (tile := tile_of(it, k, 0)) is not None:
                    e = expert_of(dve, tile)
                    if not (isinstance(tile, int) and tile < 2):
                        dve.wait_ge(inner_ready, tile - 1)
                    v.tensor_copy(w1_at[:, k % 2, :],
                                  w1_sb[:, bass.ds(e, 1), :].rearrange("p a f -> p (a f)")).then_inc(w1_ready, 1)
                if (tile := tile_of(it, k, 1)) is not None:
                    slot = (k - 1) % SLOTS
                    dve.wait_ge(xT_ready, tile + 1)
                    if not (isinstance(tile, int) and tile < SLOTS):
                        dve.wait_ge(stored[slot], (it + (k - 1) // SLOTS) * (16 * HALVES))
                    v.tensor_tensor(target[:, slot, :], x_in[:, slot, :, C],
                                    nowhere[:, at(tile), :].rearrange("p a u -> p (a u)"),
                                    ALU.min).then_inc(target_ready, 1)
                if (tile := tile_of(it, k, 2)) is not None:
                    par, slot = (k - 2) % 2, (k - 2) % SLOTS
                    e = expert_of(dve, tile)
                    if not (isinstance(tile, int) and tile < SLOTS):
                        dve.wait_ge(stored[slot], (it + (k - 2) // SLOTS) * (16 * HALVES))
                    dve.wait_ge(outer_ready, tile + 1)
                    v.tensor_tensor(o_sb[:, slot, :, :], o_ps[par][:],
                                    b2_sb[:, bass.ds(e, 1), :].to_broadcast([P, HALVES, C]),
                                    ALU.add).then_inc(o_ready, 1)
            dve.wait_ge(nowhere_in, 16)
            stages(dve, step)


def results(nc, gamma, beta, out, x_sb, m_all, weight_all, chosen_rows, eps):
    with ExitStack() as ctx:
        def sb(name, shape, dt=F32):
            return ctx.enter_context(nc.sbuf_tensor(name, shape, dt))

        def sem(name):
            return ctx.enter_context(nc.semaphore(name))

        gamma_sb = sb("gamma_sb", [P, C])
        beta_sb = sb("beta_sb", [P, C])
        got = sb("got2", [P, FETCHES, 2, GT, C])
        partial = sb("partial", [P, 2, GT, C])
        y = sb("y", [P, 2, GT, C])
        st = sb("st2", [P, GT, 6])
        mv = sb("mv2", [P, 2, GT, 2])
        sd = sb("sd2", [P, 2, GT])
        rs = sb("rs2", [P, 2, GT])
        shift = sb("shift", [P, 2, GT])
        z = sb("z", [P, 2, GT, C])
        zg = sb("zg", [P, 2, GT, C])
        xb = sb("xb", [P, 2, GT, C])
        res = sb("res", [P, 2, GT, C])

        consts_in = sem("res_consts_in")
        got_free = sem("got_free")
        fetched = [sem(f"fetched{k}") for k in range(FETCHES)]
        first_ready = sem("first_ready")
        partial_ready = sem("partial_ready")
        y_steps = sem("y_steps")
        y_stats = sem("y_stats")
        y_std = sem("y_std")
        xb_ready = sem("xb_ready")
        scale_steps = sem("scale_steps")
        scales_ready = sem("scales_ready")
        z_ready = sem("z_ready")
        zg_ready = sem("zg_ready")
        res_ready = sem("res_ready")
        out_stored = [sem(f"out_stored{k}") for k in range(2)]
        out_g = out.rearrange("b (g a p) c -> (b g) p a c", p=P, a=GT)
        chosen_g = chosen_rows[0:NOWHERE, :].rearrange("(c g a p) f -> g c p a f", c=2, a=GT, p=P)
        block = ctx.enter_context(nc.Block())

        def steps(engine, step):
            for k in range(2 * FETCHES):
                step(0, k)
            with engine.Fori(2, GROUPS // FETCHES) as it:
                for k in range(FETCHES):
                    step(it, k)
            for k in range(3):
                step(GROUPS // FETCHES, k)

        def exists(it, k, lag):
            return not isinstance(it, int) or 0 <= FETCHES * it + k - lag < GROUPS

        @block.sync
        def _(sp):
            sp.dma_start(gamma_sb[:], gamma.partition_broadcast(P)).then_inc(consts_in, 16)
            sp.dma_start(beta_sb[:], beta.partition_broadcast(P)).then_inc(consts_in, 16)
            sp.sem_inc(got_free, FETCHES)
            with sp.Fori(0, GROUPS // FETCHES) as it:
                for k in range(FETCHES):
                    i = it * FETCHES + k
                    sp.wait_ge(got_free, i + 1)
                    for c in range(2):
                        sp.dma_start(got[:, k, c, :, :], chosen_g[i, c]).then_inc(fetched[k], 16)

        @block.gpsimd
        def _(pool):
            g = nc.gpsimd

            def step(it, k):
                if exists(it, k, 3):
                    i, h = it * FETCHES + (k - 3), (k - 3) % 2
                    pool.wait_ge(xb_ready, i + 1)
                    pool.wait_ge(out_stored[h], it * (FETCHES // 2 * 16) + ((k - 3) // 2 * 16 + 16))
                    pool.wait_ge(zg_ready, i + 1)
                    g.tensor_tensor(res[:, h, :, :], zg[:, h, :, :], xb[:, h, :, :], ALU.add).then_inc(res_ready, 1)
                if exists(it, k, 0):
                    i, h = it * FETCHES + k, k % 2
                    pool.wait_ge(first_ready, i + 1)
                    g.tensor_tensor(partial[:, h, :, :], partial[:, h, :, :], m_all[:, bass.ds(i * GT, GT), :],
                                    ALU.add).then_inc(partial_ready, 1)
                if exists(it, k, 1):
                    i, h = it * FETCHES + (k - 1), (k - 1) % 2
                    if not (isinstance(i, int) and i < 2):
                        pool.wait_ge(res_ready, i - 1)
                    g.tensor_tensor(xb[:, h, :, :], x_sb[:, bass.ds(i * GT, GT), :],
                                    beta_sb[:].unsqueeze(1).to_broadcast([P, GT, C]),
                                    ALU.add).then_inc(xb_ready, 1)
            pool.wait_ge(consts_in, 32)
            steps(pool, step)

        @block.scalar
        def _(act):
            s = nc.scalar
            for h in range(2):
                act.sem_inc(out_stored[h], 16)

            def step(it, k):
                if exists(it, k, 0):
                    i, h, slot = it * FETCHES + k, k % 2, k % FETCHES
                    if not (isinstance(i, int) and i < 2):
                        act.wait_ge(y_stats, i - 1)
                    act.wait_ge(fetched[slot], it * (16 * 2) + (k // FETCHES + 1) * 16 * 2)
                    for a in range(GT):
                        ins = s.activation(partial[:, h, a, :], got[:, slot, 0, a, :], ACT.Copy,
                                           scale=weight_all[:, 0, bass.ds(i * GT + a, 1)])
                    ins.then_inc(first_ready, 1)
                if exists(it, k, 1):
                    i, h = it * FETCHES + (k - 1), (k - 1) % 2
                    act.wait_ge(y_stats, i + 1)
                    s.activation(sd[:, h, :], mv[:, h, :, 1], ACT.Sqrt, bias=eps[:]).then_inc(y_std, 1)
                if exists(it, k, 2):
                    i, h = it * FETCHES + (k - 2), k % 2
                    if not (isinstance(i, int) and i < 2):
                        act.wait_ge(zg_ready, i - 1)
                    act.wait_ge(scales_ready, i + 1)
                    for a in range(GT):
                        ins = s.activation(z[:, h, a, :], y[:, h, a, :], ACT.Identity, scale=rs[:, h, a:a + 1],
                                           bias=shift[:, h, a:a + 1])
                    ins.then_inc(z_ready, 1)
                if exists(it, k, 3):
                    i, h = it * FETCHES + (k - 3), (k - 3) % 2
                    act.wait_ge(res_ready, i + 1)
                    act.dma_start(out_g[i], res[:, h, :, :]).then_inc(out_stored[h], 16)
            steps(act, step)
            for h in range(2):
                act.wait_ge(out_stored[h], 16 * (GROUPS // 2 + 1))

        @block.vector
        def _(dve):
            v = nc.vector

            def stage_y(it, k):
                i, h, slot = it * FETCHES + (k - 1), (k - 1) % 2, (k - 1) % FETCHES
                dve.sem_clear(y_steps)
                if not (isinstance(i, int) and i < 2):
                    dve.wait_ge(z_ready, i - 1)
                dve.wait_ge(partial_ready, i + 1)
                for a in range(GT):
                    ins = v.scalar_tensor_tensor(y[:, h, a, :], got[:, slot, 1, a, :],
                                                 weight_all[:, 1, bass.ds(i * GT + a, 1)], partial[:, h, a, :],
                                                 ALU.mult, ALU.add)
                ins.then_inc(y_steps, 1)
                dve.wait_ge(y_steps, 1)
                dve.sem_inc(got_free, 1)
                for a in range(GT):
                    ins = v.bn_stats(st[:, a, :], y[:, h, a, :])
                ins.then_inc(y_steps, 1)
                dve.wait_ge(y_steps, 2)
                for a in range(GT):
                    ins = v.bn_aggr(mv[:, h, a, :], st[:, a, :])
                ins.then_inc(y_stats, 1)

            def stage_scales(it, k):
                i, h = it * FETCHES + (k - 2), k % 2
                dve.sem_clear(scale_steps)
                dve.wait_ge(y_std, i + 1)
                v.reciprocal(rs[:, h, :], sd[:, h, :]).then_inc(scale_steps, 1)
                dve.wait_ge(scale_steps, 1)
                v.scalar_tensor_tensor(shift[:, h, :], mv[:, h, :, 0], -1.0, rs[:, h, :], ALU.mult,
                                       ALU.mult).then_inc(scales_ready, 1)

            def stage_gamma(it, k):
                i, h = it * FETCHES + (k - 3), (k - 3) % 2
                if not (isinstance(i, int) and i < 2):
                    dve.wait_ge(res_ready, i - 1)
                dve.wait_ge(z_ready, i + 1)
                v.tensor_tensor(zg[:, h, :, :], z[:, h, :, :], gamma_sb[:].unsqueeze(1).to_broadcast([P, GT, C]),
                                ALU.mult).then_inc(zg_ready, 1)

            def step(it, k):
                if exists(it, k, 1):
                    stage_y(it, k)
                if exists(it, k, 3):
                    stage_gamma(it, k)
                if exists(it, k, 2):
                    stage_scales(it, k)
            dve.wait_ge(consts_in, 32)
            steps(dve, step)


INPUTS = ("x", "adj", "L0_gnn_W", "L0_gnn_b", "L0_ffn_gate_w", "L0_ffn_gate_b", "L0_ffn_w1", "L0_ffn_b1",
          "L0_ffn_w2", "L0_ffn_b2", "L0_ffn_gamma", "L0_ffn_beta")


def kernel(**inputs):
    import concourse.bacc as bacc
    from concourse.bass_utils import run_bass_kernel_spmd

    laid = {name: np.ascontiguousarray(inputs[name]) for name in INPUTS}
    laid["L0_ffn_b1"] = np.ascontiguousarray(laid["L0_ffn_b1"].reshape(E, FC, P).transpose(2, 0, 1))
    adj_t = np.ascontiguousarray(laid["adj"].reshape(B, GB, GN, N).transpose(0, 1, 3, 2).reshape(GROUPS, N, GN))
    laid = {"x": laid.pop("x"), "adj": laid.pop("adj"), "adj_t": adj_t, **laid}
    laid.update(shape_constants())
    laid.update(moe_constants())

    nc = bacc.Bacc("TRN2", target_bir_lowering=False, num_devices=1)
    args = [nc.dram_tensor(f"in_{k}", v.shape, mybir.dt.from_np(v.dtype), kind="ExternalInput").ap()
            for k, v in laid.items()]
    out = nc.dram_tensor("out", (B, N, C), F32, kind="ExternalOutput").ap()
    build(nc, *args, out)
    r = run_bass_kernel_spmd(nc, [{f"in_{k}": v for k, v in laid.items()}], core_ids=[0])
    return r.results[0]["out"]
```
